# Optimizing a Trainium2 kernel written in Bass

```python
import numpy as np
import jax
import jax.numpy as jnp

def _softmax(x, axis=-1):
    return jax.nn.softmax(x, axis=axis)

def _gelu(x):
    return jax.nn.gelu(x, approximate=True)

def _silu(x):
    return jax.nn.silu(x)

def _sigmoid(x):
    return jax.nn.sigmoid(x)

def _layernorm(x, axis=-1, eps=1e-05):
    m = jnp.mean(x, axis=axis, keepdims=True)
    v = jnp.var(x, axis=axis, keepdims=True)
    return (x - m) / jnp.sqrt(v + eps)

def _scatter_add(tgt, idx, src, axis=0):
    return tgt.at[idx].add(src)

def _segment_sum(src, seg, n):
    return jax.ops.segment_sum(src, seg, n)
kernel_name = 'mk_audio_tower_d1_tok_audfeat512_r4_c40982'

def setup_inputs(seed: int=0):
    np.random.seed(seed)
    _w = jnp.asarray

    def _rec_inputs():
        import jax
        import jax.numpy as jnp
        _rk = jax.random.key(seed)
        x = -0.000392918 + 0.999932 * jax.random.normal(jax.random.fold_in(_rk, 1), (64, 125, 128), jnp.float32)
        return x
    x = _rec_inputs()

    def _L0_tok_setup():
        import jax, jax.numpy as jnp
        import numpy as np
        B, T, D, H = (8, 1024, 128, 128)

        def _linear_params(key, d_in, d_out):
            k1, k2 = jax.random.split(key)
            bound = 1.0 / np.sqrt(d_in)
            W = jax.random.uniform(k1, (d_in, d_out), jnp.float32, -bound, bound)
            b = jax.random.uniform(k2, (d_out,), jnp.float32, -bound, bound)
            return (W, b)

        def _log_g(z):
            return jnp.where(z >= 0, jnp.log(jax.nn.relu(z) + 0.5), -jax.nn.softplus(-z))
        key = jax.random.key(seed)
        kx, kf, ki, kh = jax.random.split(key, 4)
        x = jax.random.normal(kx, (B, T, D), dtype=jnp.float32)
        Wf, bf = _linear_params(kf, D, H)
        Wi, bi = _linear_params(ki, D, H)
        Wh, bh = _linear_params(kh, D, H)
        return {'x': x, 'Wf': Wf, 'bf': bf, 'Wi': Wi, 'bi': bi, 'Wh': Wh, 'bh': bh}
    _L0_tok_all = _L0_tok_setup()
    _L0_tok_in = {k: v for k, v in _L0_tok_all.items() if k in ('Wf', 'bf', 'Wi', 'bi', 'Wh', 'bh')}
    del _L0_tok_all

    def _L0_attn_setup():
        import jax, jax.numpy as jnp
        import numpy as np
        S, B, H, D, IN = (128, 8, 8, 64, 128)
        PROJ = H * (5 * D + 2)
        key = jax.random.key(seed)
        k0, k1, k2 = jax.random.split(key, 3)
        x = jax.random.normal(k0, (S, B, IN), jnp.float32)
        W_slow = jax.random.normal(k1, (PROJ, IN), jnp.float32) / np.sqrt(IN).astype(np.float32)
        W_out = jax.random.normal(k2, (IN, H * D), jnp.float32) / np.sqrt(H * D).astype(np.float32)
        ln_gamma = jnp.ones((IN,), jnp.float32)
        ln_beta = jnp.zeros((IN,), jnp.float32)
        return dict(x=x, W_slow=W_slow, W_out=W_out, ln_gamma=ln_gamma, ln_beta=ln_beta)
    _L0_attn_all = _L0_attn_setup()
    _L0_attn_in = {k: v for k, v in _L0_attn_all.items() if k in ('W_slow', 'W_out', 'ln_gamma', 'ln_beta')}
    del _L0_attn_all

    def _L0_ffn_setup():
        import jax, jax.numpy as jnp
        import numpy as np
        FP8_MAX = 448.0
        K, N = (128, 128)
        key = jax.random.key(seed)
        kx, kw = jax.random.split(key)
        x = jax.random.normal(kx, (8, 2048, K), dtype=jnp.float32)
        weight = jax.random.normal(kw, (K, N), dtype=jnp.float32) * 0.02
        return {'x': x, 'weight': weight}
    _L0_ffn_all = _L0_ffn_setup()
    _L0_ffn_in = {k: v for k, v in _L0_ffn_all.items() if k in ('weight',)}
    del _L0_ffn_all
    return {'x': x, 'L0_tok_Wf': _L0_tok_in['Wf'], 'L0_tok_bf': _L0_tok_in['bf'], 'L0_tok_Wi': _L0_tok_in['Wi'], 'L0_tok_bi': _L0_tok_in['bi'], 'L0_tok_Wh': _L0_tok_in['Wh'], 'L0_tok_bh': _L0_tok_in['bh'], 'L0_attn_W_slow': _L0_attn_in['W_slow'], 'L0_attn_W_out': _L0_attn_in['W_out'], 'L0_attn_ln_gamma': _L0_attn_in['ln_gamma'], 'L0_attn_ln_beta': _L0_attn_in['ln_beta'], 'L0_ffn_weight': _L0_ffn_in['weight']}

def reference(x, L0_tok_Wf, L0_tok_bf, L0_tok_Wi, L0_tok_bi, L0_tok_Wh, L0_tok_bh, L0_attn_W_slow, L0_attn_W_out, L0_attn_ln_gamma, L0_attn_ln_beta, L0_ffn_weight):
    import jax
    import jax.numpy as jnp

    def _L0_tok_ref(x, Wf, bf, Wi, bi, Wh, bh):
        import jax, jax.numpy as jnp
        import numpy as np
        B, T, D, H = (8, 1024, 128, 128)

        def _linear_params(key, d_in, d_out):
            k1, k2 = jax.random.split(key)
            bound = 1.0 / np.sqrt(d_in)
            W = jax.random.uniform(k1, (d_in, d_out), jnp.float32, -bound, bound)
            b = jax.random.uniform(k2, (d_out,), jnp.float32, -bound, bound)
            return (W, b)

        def _log_g(z):
            return jnp.where(z >= 0, jnp.log(jax.nn.relu(z) + 0.5), -jax.nn.softplus(-z))
        b, t, h = (x.shape[0], x.shape[1], Wf.shape[1])
        zf = x @ Wf + bf
        zi = x @ Wi + bi
        zh = x @ Wh + bh
        diff = jax.nn.softplus(-zf) - jax.nn.softplus(-zi)
        log_f = -jax.nn.softplus(diff)
        log_i = -jax.nn.softplus(-diff)
        log_h0 = jnp.full((b, 1, h), jnp.log(jnp.float32(0.5)), dtype=x.dtype)
        log_tilde_h = _log_g(zh)
        log_val = jnp.concatenate([log_h0, log_i + log_tilde_h], axis=1)
        a_star = jnp.concatenate([jnp.zeros((b, 1, h), dtype=x.dtype), log_f], axis=1)
        log_h = a_star + jax.lax.cumlogsumexp(log_val - a_star, axis=1)
        return jnp.exp(log_h)

    def _L0_attn_ref(x, W_slow, W_out, ln_gamma, ln_beta):
        import jax, jax.numpy as jnp
        import numpy as np
        S, B, H, D, IN = (128, 8, 8, 64, 128)
        PROJ = H * (5 * D + 2)
        slen, bsz, in_dim = x.shape
        mu = x.mean(-1, keepdims=True)
        var = x.var(-1, keepdims=True)
        normed = (x - mu) / jnp.sqrt(var + 1e-05) * ln_gamma + ln_beta
        qkvb = (normed @ W_slow.T).reshape(slen, bsz, H, 5 * D + 2)
        q, k, v, rk, rv, beta, rbeta = jnp.split(qkvb, [D, 2 * D, 3 * D, 4 * D, 5 * D, 5 * D + 1], axis=-1)
        q = jax.nn.softmax(q, axis=-1)
        k = jax.nn.softmax(k, axis=-1)
        rk = jax.nn.softmax(rk, axis=-1)
        beta = jax.nn.sigmoid(beta)
        rbeta = jax.nn.sigmoid(rbeta)
        W0 = jnp.zeros((bsz, H, D, D), x.dtype)

        def fw_step(W, inp):
            qt, kt, vt, bt = inp
            v_old = jnp.einsum('bhij,bhj->bhi', W, kt)
            W = W + (bt * (vt - v_old))[..., :, None] * kt[..., None, :]
            z = jnp.einsum('bhij,bhj->bhi', W, qt)
            return (W, z)
        _, z = jax.lax.scan(fw_step, W0, (q, k, v, beta))
        R0 = jnp.zeros((bsz, H, D, D), x.dtype)
        h0 = jnp.zeros((bsz, H, D), x.dtype)

        def rec_step(carry, inp):
            R, h = carry
            zt, kt, vt, bt = inp
            qh = jax.nn.softmax(h, axis=-1)
            v_old = jnp.einsum('bhij,bhj->bhi', R, kt)
            R = R + (bt * (vt - v_old))[..., :, None] * kt[..., None, :]
            h = zt + jnp.einsum('bhij,bhj->bhi', R, qh)
            return ((R, h), h)
        _, hs = jax.lax.scan(rec_step, (R0, h0), (z, rk, rv, rbeta))
        out = hs.reshape(slen, bsz, H * D) @ W_out.T
        return x + out

    def _L0_ffn_ref(x, weight):
        import jax, jax.numpy as jnp
        import numpy as np
        FP8_MAX = 448.0
        K, N = (128, 128)
        B, S, _ = x.shape
        x2d = x.reshape(-1, K)
        x_amax = jnp.max(jnp.abs(x2d))
        x_scale = FP8_MAX / jnp.maximum(x_amax, 1e-12)
        x_fp8 = jnp.clip(x2d * x_scale, -FP8_MAX, FP8_MAX).astype(jnp.float8_e4m3fn)
        w_amax = jnp.max(jnp.abs(weight))
        w_scale = FP8_MAX / jnp.maximum(w_amax, 1e-12)
        w_fp8 = jnp.clip(weight.T * w_scale, -FP8_MAX, FP8_MAX).astype(jnp.float8_e4m3fn)
        res = jnp.matmul(x_fp8.astype(jnp.float32), w_fp8.astype(jnp.float32).T)
        out = res * (1.0 / x_scale * (1.0 / w_scale))
        return out.reshape(B, S, N).astype(x.dtype)
    h = _L0_tok_ref(x, L0_tok_Wf, L0_tok_bf, L0_tok_Wi, L0_tok_bi, L0_tok_Wh, L0_tok_bh)
    h = h + _L0_attn_ref(_layernorm(h, axis=-1), L0_attn_W_slow, L0_attn_W_out, L0_attn_ln_gamma, L0_attn_ln_beta)
    h = h + _L0_ffn_ref(_layernorm(h, axis=-1), L0_ffn_weight)
    return h

_drawn_inputs = setup_inputs


def setup_inputs(seed=0):
    import zlib

    import numpy as np

    out = dict(_drawn_inputs(seed))
    spreads = {'L0_attn_ln_gamma': (1.0, 0.6), 'L0_attn_ln_beta': (0.0, 0.8)}
    factors = {'L0_tok_bf': 3.091,
     'L0_tok_bi': 4.316,
     'L0_attn_W_slow': 8.0,
     'L0_attn_W_out': 8.0,
     'L0_ffn_weight': 6.824}
    for name, (base, spread) in spreads.items():
        noise = np.random.default_rng([zlib.crc32(name.encode()), seed]).standard_normal(out[name].shape)
        drawn = base * np.exp(spread * noise) if base else spread * noise
        out[name] = jnp.asarray(drawn.astype(out[name].dtype))
    for name, factor in factors.items():
        out[name] = (out[name] * factor).astype(out[name].dtype)
    return out
```

```python
import concourse.bass as bass
from concourse import mybir
from contextlib import ExitStack

F32 = mybir.dt.float32
BF16 = mybir.dt.bfloat16
U32 = mybir.dt.uint32
ALU = mybir.AluOpType
ACT = mybir.ActivationFunctionType
AX = mybir.AxisListType

N = 64
T = 125
TT = T + 1
TP = 128
C = 128
H, D = 8, 64
HD = H * D
PR = 5 * D + 2
NT = TP // 2
NS = NT // 2
EPS = 1e-5
CUT = 40.0
FP8_MAX = 448.0
HP = 2


class Tally:

    def __init__(self, eng, sem, start=0):
        self.eng, self.sem, self.n, self.start = eng, sem, 0, start

    def __call__(self, ins):
        ins.then_inc(self.sem, 1)
        self.n += 1

    def wait(self):
        self.eng.wait_ge(self.sem, self.start + self.n)

    def link(self, ins):
        self(ins)
        self.wait()


def apart(eng, sem):
    eng.sem_inc(sem, 1)


def audio_layer(nc, x, Wf, bf, Wi, bi, Wh, bh, W_slow, W_out, gamma, beta, weight, out):
    k_scr = nc.dram_tensor("k_scr", (TP, N, HD), F32, kind="Internal").ap()
    y_scr = nc.dram_tensor("y_scr", (TP, N, HD), F32, kind="Internal").ap()
    z_scr = nc.dram_tensor("z_scr", (TP, N, HD), F32, kind="Internal").ap()

    ctx = ExitStack()
    with ctx:
        def keep(name, shape, dt=F32):
            return ctx.enter_context(nc.sbuf_tensor(name, shape, dt))

        ident = keep("ident", [128, 128])
        identb = keep("identb", [128, 128], BF16)
        ones = keep("ones", [128, 128])
        consts = keep("consts", [128, 4])
        zero, one, eps, bhh = (consts[:, k:k + 1] for k in range(4))
        woT = keep("woT", [C, 4, C])
        wq = keep("wq", [C, C], BF16)
        wmax = keep("wmax", [128, 1])
        res = keep("res", [128, NT, C])
        build_weights_and_mid(nc, locals())
        recurrence(nc, k_scr, y_scr, z_scr)
        finish(nc, locals())


def build_weights_and_mid(nc, v):
    ident, identb, ones, consts, zero, one, eps, bhh, woT, wq, wmax, res = (
        v[k] for k in "ident identb ones consts zero one eps bhh woT wq wmax res".split())
    with ExitStack() as c:
        def sb(name, shape, dt=F32):
            return c.enter_context(nc.sbuf_tensor(name, shape, dt))
        wsT = sb("wsT", [C, 5 * HD + 2 * H])
        gates = sb("gates", [C, 3, C])
        biases = sb("biases", [C, 8])
        gam, bet = sb("gam", [C, 1]), sb("bet", [C, 1])
        hT = sb("hT", [C, N, TP])
        maskP = sb("maskP", [128, 128])
        weights(nc, v, wsT, gates, biases, gam, bet, hT, maskP)
        mingru(nc, v, gates, biases, hT)
        attention_setup(nc, v, wsT, gam, bet, hT, maskP)


def weights(nc, v, wsT, gates, biases, gam, bet, hT, maskP):
    ident, identb, ones, consts, woT, wq, wmax = (v[k] for k in "ident identb ones consts woT wq wmax".split())
    W_slow, W_out = v["W_slow"], v["W_out"]
    with ExitStack() as c:
        def sb(name, shape, dt=F32):
            return c.enter_context(nc.sbuf_tensor(name, shape, dt))

        def sem(name):
            return c.enter_context(nc.semaphore(name))
        rows = sb("rows", [128, 5, 4, C])
        brows = sb("brows", [2 * H, C])
        worows = sb("worows", [C, HD])
        w8 = sb("w8", [C, C])
        q8 = sb("q8", [C, 3, C])
        st = sb("st", [128, 8])
        banks = [c.enter_context(nc.psum_tensor(f"turn{k}", [128, 512], F32)) for k in range(8)]
        loaded, consts_set, turned, copied, chain = (sem(s) for s in (
            "loaded", "consts_set", "turned", "copied", "w8_step"))
        amax_t, amax_b = sem("amax_turned"), sem("amax_spread")
        per_head = W_slow.rearrange("(h r) c -> h r c", r=PR)
        block = c.enter_context(nc.Block())
        NLOAD = 10 + 2 + 1 + 1 + 3 + 3 + 2

        @block.sync
        def _(sp):
            for kind in range(5):
                for par in range(2):
                    sp.dma_start(rows[D * par:D * par + D, kind, :, :],
                                 per_head[par::2, kind * D:(kind + 1) * D, :].rearrange("h d c -> d h c")
                                 ).then_inc(loaded, 16)
            for r in range(2):
                sp.dma_start(brows[H * r:H * r + H, :], per_head[:, 5 * D + r, :]).then_inc(loaded, 16)
            sp.dma_start(worows[:, :], W_out).then_inc(loaded, 16)
            sp.dma_start(w8[:, :], v["weight"]).then_inc(loaded, 16)
            for k, name in enumerate(("Wf", "Wi", "Wh")):
                sp.dma_start(gates[:, k, :], v[name]).then_inc(loaded, 16)
            for k, name in enumerate(("bf", "bi", "bh")):
                sp.dma_start(biases[:, k:k + 1], v[name].rearrange("(p a) -> p a", a=1)).then_inc(loaded, 16)
            sp.dma_start(gam[:, :], v["gamma"].rearrange("(p a) -> p a", a=1)).then_inc(loaded, 16)
            sp.dma_start(bet[:, :], v["beta"].rearrange("(p a) -> p a", a=1)).then_inc(loaded, 16)

        @block.gpsimd
        def _(pool):
            step = Tally(pool, consts_set)
            step(pool.memset(ident[:, :], 0.0))
            step(pool.memset(maskP[:, :], 1.0))
            step(pool.memset(ones[:, :], 1.0))
            step(pool.memset(consts[:, 0:1], 0.0))
            step(pool.memset(consts[:, 1:2], 1.0))
            step(pool.memset(consts[:, 2:3], EPS))
            step(pool.memset(hT[:, :, :], 0.0))
            step.wait()
            step.link(pool.affine_select(out=ident[:, :], in_=ident[:, :], compare_op=ALU.not_equal, fill=1.0,
                                         base=0, pattern=[[-1, 128]], channel_multiplier=1))
            step.link(pool.affine_select(out=maskP[:, :], in_=maskP[:, :], compare_op=ALU.is_ge, fill=0.0,
                                         base=0, pattern=[[1, 128]], channel_multiplier=-1))
            step.link(pool.affine_select(out=maskP[:, N:], in_=maskP[:, N:], compare_op=ALU.is_ge, fill=0.0,
                                         base=-N, pattern=[[0, N]], channel_multiplier=1))

        @block.tensor
        def _(pe):
            pe.wait_ge(loaded, 16 * NLOAD)
            pe.wait_ge(consts_set, 10)
            for kind in range(5):
                for hp in range(4):
                    ins = pe.transpose(banks[kind][:, hp * 128:(hp + 1) * 128], rows[:, kind, hp, :], ident[:, :])
            pe.transpose(banks[5][:, 0:2 * H], brows[:, :], ident[0:2 * H, 0:2 * H])
            for k in range(4):
                ins = pe.transpose(banks[6][:, k * 128:(k + 1) * 128], worows[:, k * 128:(k + 1) * 128], ident[:, :])
            ins.then_inc(turned, 1)
            pe.wait_ge(chain, 1)
            pe.transpose(banks[7][0:1, 0:128], st[:, 0:1], ident[:, :]).then_inc(amax_t, 1)
            pe.wait_ge(chain, 2)
            pe.matmul(banks[7][:, 128:129], ones[0:1, :], st[0:1, 1:2], start=True, stop=True).then_inc(amax_b, 1)

        @block.scalar
        def _(act):
            act.wait_ge(turned, 1)
            for kind in range(5):
                act.activation(wsT[:, kind * HD:(kind + 1) * HD], banks[kind][:, :], ACT.Copy)
            act.activation(wsT[:, 5 * HD:], banks[5][:, 0:2 * H], ACT.Copy)
            act.activation(woT[:, :, :].rearrange("p a b -> p (a b)"), banks[6][:, :], ACT.Copy).then_inc(copied, 1)
            act.wait_ge(copied, 1)

        @block.vector
        def _(dve):
            step = Tally(dve, chain)
            dve.wait_ge(loaded, 16 * NLOAD)
            step(dve.tensor_reduce(st[:, 0:1], w8[:, :], AX.X, ALU.max, apply_absolute_value=True))
            dve.wait_ge(amax_t, 1)
            step(dve.tensor_reduce(st[0:1, 1:2], banks[7][0:1, 0:128], AX.X, ALU.max))
            dve.wait_ge(amax_b, 1)
            step.link(dve.tensor_scalar(wmax[:, :], banks[7][:, 128:129], 1e-12, None, ALU.max))
            step.link(dve.reciprocal(st[:, 2:3], wmax[:, :]))
            step.link(dve.tensor_scalar(st[:, 3:4], st[:, 2:3], FP8_MAX, None, ALU.mult))
            quantise(dve, step, wq[:, :], w8[:, :], st[:, 3:4], q8)
            dve.wait_ge(consts_set, 10)
            step.link(dve.tensor_scalar(biases[:, 3:6], biases[:, 0:3], -1.0, None, ALU.mult))
            step.link(dve.tensor_scalar(consts[:, 3:4], biases[:, 2:3], 0.5, None, ALU.add))
            step.link(dve.tensor_copy(identb[:, :], ident[:, :]))


def quantise(dve, step, to, src, scale, q):
    step.link(dve.tensor_scalar(q[:, 0, :], src, scale, FP8_MAX, ALU.mult, ALU.min))
    step.link(dve.tensor_scalar(q[:, 0, :], q[:, 0, :], -FP8_MAX, None, ALU.max))
    step.link(dve.tensor_scalar(q[:, 1, :].bitcast(U32), q[:, 0, :].bitcast(U32), 0x7F800000, None, ALU.bitwise_and))
    step.link(dve.tensor_scalar(q[:, 1, :], q[:, 1, :], 2.0 ** -6, 1.5 * 2.0 ** 20, ALU.max, ALU.mult))
    step.link(dve.tensor_tensor(q[:, 2, :], q[:, 0, :], q[:, 1, :], ALU.add))
    step.link(dve.tensor_tensor(to, q[:, 2, :], q[:, 1, :], ALU.subtract))



def mingru(nc, v, gates, biases, hT):
    ident, one, bhh = v["ident"], v["one"], v["bhh"]
    G = 4
    NG = N // G
    W = G * T
    nbh = biases[:, 5:6]
    with ExitStack() as c:
        def sb(name, shape, dt=F32):
            return c.enter_context(nc.sbuf_tensor(name, shape, dt))

        def sem(name):
            return c.enter_context(nc.semaphore(name))

        def pb(name):
            return c.enter_context(nc.psum_tensor(name, [128, 512], F32))
        xin = [sb(f"xin{b}", [T, G, C]) for b in range(2)]
        xT = [sb(f"xT{b}", [C, W]) for b in range(2)]
        px = [pb(f"px{b}") for b in range(2)]
        pz = [[pb(f"pz{b}{k}") for k in range(3)] for b in range(2)]
        zc = [sb(f"zc{b}", [C, 2, W]) for b in range(2)]
        zr = [sb(f"zr{b}", [C, 2, W]) for b in range(2)]
        ex = [sb(f"ex{b}", [C, 2, W]) for b in range(2)]
        sp_ = [sb(f"softp{b}", [C, 2, W]) for b in range(2)]
        df = [sb(f"diff{b}", [C, W]) for b in range(2)]
        dc = [sb(f"diffc{b}", [C, W]) for b in range(2)]
        ld = [sb(f"ld{b}", [C, W]) for b in range(2)]
        sd = [sb(f"sd{b}", [C, G, TT]) for b in range(2)]
        la = [sb(f"la{b}", [C, 2, W]) for b in range(2)]
        eh = [sb(f"eh{b}", [C, W]) for b in range(2)]
        sg = [sb(f"sg{b}", [C, W]) for b in range(2)]
        aa = [sb(f"aa{b}", [C, G, TT]) for b in range(2)]
        ib = [sb(f"ib{b}", [C, W]) for b in range(2)]
        bb = [sb(f"bb{b}", [C, G, TT]) for b in range(2)]
        x_in = [sem(f"x_in{b}") for b in range(2)]
        x_turned, x_copied, z_made, act_step, dve_step, pool_step, edge, s_apart = (sem(s) for s in (
            "x_turned", "x_copied", "z_made", "gru_act", "gru_dve", "gru_pool", "edges", "waited"))
        AS, DS, PS = 7, 9, 6
        block = c.enter_context(nc.Block())

        @block.sync
        def _(sp):
            with sp.Fori(0, NG // 2) as i:
                for b in range(2):
                    sp.wait_ge(x_turned, i * 2)
                    apart(sp, s_apart)
                    sp.dma_start(xin[b][:, :, :], v["x"][bass.ds(i * (2 * G) + b * G, G), :, :]
                                 .rearrange("g t c -> t g c")).then_inc(x_in[b], 16)

        @block.tensor
        def _(pe):
            with pe.Fori(0, NG // 2) as i:
                for b in range(2):
                    g = i * 2 + b
                    pe.wait_ge(x_in[b], i * 16 + 16)
                    pe.wait_ge(x_copied, g)
                    for k in range(G):
                        ins = pe.transpose(px[b][:, k * T:(k + 1) * T], xin[b][:, k, :], ident[0:T, 0:T])
                    ins.then_inc(x_turned, 1)
                    pe.wait_ge(x_copied, g + 1)
                    pe.wait_ge(act_step, g * AS)
                    pe.wait_ge(dve_step, g * DS)
                    for k in range(3):
                        ins = pe.matmul(pz[b][k][:, 0:W], gates[:, k, :], xT[b][:, :], start=True, stop=True)
                    ins.then_inc(z_made, 1)

        @block.scalar
        def _(act):
            with act.Fori(0, NG // 2) as i:
                for b in range(2):
                    g = i * 2 + b
                    a0, d0, p0 = g * AS, g * DS, g * PS
                    act.wait_ge(x_turned, g + 1)
                    act.wait_ge(z_made, g)
                    act.activation(xT[b][:, :], px[b][:, 0:W], ACT.Copy).then_inc(x_copied, 1)
                    act.wait_ge(z_made, g + 1)
                    act.wait_ge(pool_step, p0)
                    act.activation(eh[b][:, :], pz[b][2][:, 0:W], ACT.Exp, bias=nbh, scale=-1.0).then_inc(act_step, 1)
                    act.wait_ge(dve_step, d0 + 2)
                    act.activation(ex[b][:, :, :], zc[b][:, :, :], ACT.Exp, scale=-1.0).then_inc(act_step, 1)
                    act.wait_ge(act_step, a0 + 2)
                    act.activation(sp_[b][:, :, :], ex[b][:, :, :], ACT.Ln, bias=one).then_inc(act_step, 1)
                    act.wait_ge(dve_step, d0 + 5)
                    act.activation(ld[b][:, :], dc[b][:, :], ACT.Exp).then_inc(act_step, 1)
                    act.wait_ge(act_step, a0 + 4)
                    act.activation(ld[b][:, :], ld[b][:, :], ACT.Ln, bias=one).then_inc(act_step, 1)
                    act.wait_ge(pool_step, p0 + 6)
                    act.activation(aa[b][:, :, 1:TT], la[b][:, 0, :].rearrange("p (g t) -> p g t", g=G), ACT.Exp
                                   ).then_inc(act_step, 1)
                    act.activation(ib[b][:, :], la[b][:, 1, :], ACT.Exp).then_inc(act_step, 1)

        @block.vector
        def _(dve):
            for b in range(2):
                dve.memset(aa[b][:, :, 0:1], 0.0)
                dve.memset(bb[b][:, :, 0:1], 0.5)
                dve.memset(sd[b][:, :, 0:1], 0.0).then_inc(edge, 1)
            dve.wait_ge(edge, 2)
            with dve.Fori(0, NG // 2) as i:
                for b in range(2):
                    g = i * 2 + b
                    a0, d0, p0 = g * AS, g * DS, g * PS
                    dve.wait_ge(z_made, g + 1)
                    dve.wait_ge(pool_step, p0)
                    for k in range(2):
                        dve.tensor_scalar(zc[b][:, k, :], pz[b][k][:, 0:W], biases[:, k:k + 1], -CUT,
                                          ALU.add, ALU.max).then_inc(dve_step, 1)
                    for k in range(2):
                        dve.wait_ge(dve_step, d0 + 1 + k)
                        dve.scalar_tensor_tensor(out=zr[b][:, k, :], in0=pz[b][k][:, 0:W], scalar=biases[:, k:k + 1],
                                                 in1=zc[b][:, k, :], op0=ALU.add, op1=ALU.subtract
                                                 ).then_inc(dve_step, 1)
                    dve.wait_ge(pool_step, p0 + 2)
                    dve.tensor_scalar(dc[b][:, :], df[b][:, :], CUT, None, ALU.min).then_inc(dve_step, 1)
                    dve.wait_ge(act_step, a0 + 1)
                    dve.tensor_scalar(eh[b][:, :], eh[b][:, :], 1.0, None, ALU.add).then_inc(dve_step, 1)
                    dve.wait_ge(dve_step, d0 + 6)
                    dve.reciprocal(sg[b][:, :], eh[b][:, :]).then_inc(dve_step, 1)
                    dve.wait_ge(dve_step, d0 + 7)
                    dve.scalar_tensor_tensor(out=sg[b][:, :], in0=pz[b][2][:, 0:W], scalar=bhh,
                                             in1=sg[b][:, :], op0=ALU.add, op1=ALU.max).then_inc(dve_step, 1)
                    dve.wait_ge(dve_step, d0 + 8)
                    dve.wait_ge(act_step, a0 + 7)
                    dve.tensor_tensor(bb[b][:, :, 1:TT], ib[b][:, :].rearrange("p (g t) -> p g t", g=G),
                                      sg[b][:, :].rearrange("p (g t) -> p g t", g=G), ALU.mult).then_inc(edge, 1)
                    dve.wait_ge(edge, g + 3)
                    for s in range(G):
                        ins = dve.tensor_tensor_scan(hT[:, bass.ds(g * G + s, 1), 0:TT].rearrange("p a t -> p (a t)"),
                                                     aa[b][:, s, :], bb[b][:, s, :], 0.0, ALU.mult, ALU.add)
                    ins.then_inc(dve_step, 1)

        @block.gpsimd
        def _(pool):
            pool.wait_ge(edge, 2)
            with pool.Fori(0, NG // 2) as i:
                for b in range(2):
                    g = i * 2 + b
                    a0, d0, p0 = g * AS, g * DS, g * PS
                    pool.wait_ge(act_step, a0 + 3)
                    pool.wait_ge(dve_step, d0 + 4)
                    pool.tensor_tensor(sp_[b][:, :, :], sp_[b][:, :, :], zr[b][:, :, :], ALU.subtract).then_inc(pool_step, 1)
                    pool.wait_ge(pool_step, p0 + 1)
                    pool.tensor_tensor(df[b][:, :], sp_[b][:, 0, :], sp_[b][:, 1, :], ALU.subtract).then_inc(pool_step, 1)
                    pool.wait_ge(dve_step, d0 + 5)
                    pool.wait_ge(act_step, a0 + 5)
                    pool.tensor_tensor(zr[b][:, 0, :], df[b][:, :], dc[b][:, :], ALU.subtract).then_inc(pool_step, 1)
                    pool.wait_ge(pool_step, p0 + 3)
                    pool.tensor_tensor(sd[b][:, :, 1:TT], ld[b][:, :].rearrange("p (g t) -> p g t", g=G),
                                       zr[b][:, 0, :].rearrange("p (g t) -> p g t", g=G), ALU.add).then_inc(pool_step, 1)
                    pool.wait_ge(pool_step, p0 + 4)
                    pool.tensor_tensor(la[b][:, 0, :].rearrange("p (g t) -> p g t", g=G), sd[b][:, :, 0:T],
                                       sd[b][:, :, 1:TT], ALU.subtract).then_inc(pool_step, 1)
                    pool.tensor_tensor(la[b][:, 1, :].rearrange("p (g t) -> p g t", g=G),
                                       df[b][:, :].rearrange("p (g t) -> p g t", g=G),
                                       sd[b][:, :, 1:TT], ALU.subtract).then_inc(pool_step, 1)


class Bank:

    def __init__(self, tensor, full, free, uses):
        self.t, self.full, self.free, self.uses = tensor, full, free, uses.split()

    def wait_free(self, pe, i, use):
        pe.wait_ge(self.free, i * len(self.uses) + self.uses.index(use))

    def wait_emptied(self, eng, i, use):
        eng.wait_ge(self.free, i * len(self.uses) + self.uses.index(use) + 1)

    def wait_full(self, eng, i, use):
        eng.wait_ge(self.full, i * len(self.uses) + self.uses.index(use) + 1)


def attention_setup(nc, v, wsT, gam, bet, hT, maskP):
    ident, one, eps, res = v["ident"], v["one"], v["eps"], v["res"]
    k_scr, y_scr, z_scr = v["k_scr"], v["y_scr"], v["z_scr"]
    B = 32
    U = 2 * 2 * H
    with ExitStack() as c:
        def sb(name, shape, dt=F32):
            return c.enter_context(nc.sbuf_tensor(name, shape, dt))

        def sem(name):
            return c.enter_context(nc.semaphore(name))

        def bank(k, uses):
            return Bank(c.enter_context(nc.psum_tensor(f"bank{k}", [128, 512], F32)),
                        sem(f"full{k}"), sem(f"free{k}"), uses)
        pair = range(2)
        hcol = [sb(f"hcol{g}", [C, 128]) for g in pair]
        stats = [sb(f"stats{g}", [128, 6]) for g in pair]
        mv = [sb(f"mv{g}", [128, 4]) for g in pair]
        rstd = [sb(f"rstd{g}", [128, 4]) for g in pair]
        yln = [sb(f"yln{g}", [128, C]) for g in pair]
        yn = [sb(f"yn{g}", [128, C]) for g in pair]
        nT = [sb(f"nT{g}", [C, 128]) for g in pair]
        sbeta = [sb(f"sbeta{g}", [128, 2 * H]) for g in pair]
        bcut = [sb(f"bcut{g}", [128, 2, 2 * H]) for g in pair]
        nmax = sb("nmax", [128, 3 * H])
        ek = [sb(f"ek{k}", [128, H, D]) for k in range(3)]
        sums = [sb(f"sums{g}", [128, 3 * H]) for g in pair]
        cc = [sb(f"cc{g}", [128, 3 * H]) for g in pair]
        kt = [[sb(f"kt{g}{k}", [128, H, D]) for k in range(3)] for g in pair]
        kT = [[sb(f"kT{g}{k}", [128, 4, 128]) for k in range(3)] for g in pair]
        rhs = [sb(f"rhs{g}", [128, 2 * H, D]) for g in pair]
        lin = sb("lin", [128, B, U])
        lt = sb("lt", [128, B, B])
        xi = sb("xi", [128, B, B])
        prod = sb("prod", [128, B * B // 4])
        xid = sb("xid", [128, B, B])
        xT = sb("xT", [128, B, U])
        cexp = [sb(f"cexp{g}", [128, 2 * H, 128]) for g in pair]
        xexp = sb("xexp", [128, U, 128])
        pexp = [sb(f"pexp{g}", [128, H, 128]) for g in pair]
        yi = [sb(f"yi{g}", [128, 2 * H, D]) for g in pair]
        yf = [sb(f"yf{g}", [128, 2 * H, D]) for g in pair]
        zf = [sb(f"zf{g}", [128, H, D]) for g in pair]
        b0 = bank(0, "ph0 ph1 z0 z1")
        b1 = bank(1, "pn0 pn1 be0 be1 P0 P1")
        b2 = bank(2, "q0 q1 Tq0 Tq1 ya0 ya1")
        b3 = bank(3, "k0 k1 Tk0 Tk1 yb0 yb1")
        b4 = bank(4, "r0 r1 Tr0 Tr1 ca0 ca1")
        b5 = bank(5, "v0 v1 A0 A1 cb0 cb1")
        b6 = bank(6, "w0 w1 A0 A1 fa0 fa1")
        b7 = bank(7, "P0 P1 fb0 fb1")
        (s_hcol, s_var1, s_rstd1, s_var2, s_rstd2, s_yn, s_blog, s_bsum, s_sbeta, s_e, s_cc, s_kt, s_xT, s_xexp,
         s_xi, s_apart, s_zeroed, s_dve, s_act) = (sem(s) for s in (
            "hcol_ready var1_ready rstd1_ready var2_ready rstd2_ready yn_ready beta_log beta_softplus sbeta_ready e_ready "
            "scales_ready kt_ready xT_ready xexp_ready xi_reset waited zeroed dve_step act_step").split())
        k_stored = [sem(f"k_stored{g}") for g in pair]
        y_stored = [sem(f"y_stored{g}") for g in pair]
        z_stored = [sem(f"z_stored{g}") for g in pair]
        block = c.enter_context(nc.Block())

        @block.sync
        def _(sp):
            with sp.Fori(0, NS) as i:
                for g in pair:
                    t = i * 2 + g
                    taus = bass.ds(i * 4 + 2 * g, 2)
                    sp.wait_ge(s_kt, t * 3 + 3)
                    apart(sp, s_apart)
                    sp.dma_start(k_scr[taus, :, :].rearrange("a n c -> (a n) c"),
                                 kt[g][2][:, :, :].rearrange("p h d -> p (h d)")).then_inc(k_stored[g], 16)
                for g in pair:
                    t = i * 2 + g
                    taus = bass.ds(i * 4 + 2 * g, 2)
                    b7.wait_emptied(sp, i, f"fb{g}")
                    apart(sp, s_apart)
                    sp.dma_start(y_scr[taus, :, :].rearrange("a n c -> (a n) c"),
                                 yf[g][:, H:, :].rearrange("p h d -> p (h d)")).then_inc(y_stored[g], 16)
                for g in pair:
                    t = i * 2 + g
                    taus = bass.ds(i * 4 + 2 * g, 2)
                    b0.wait_emptied(sp, i, f"z{g}")
                    apart(sp, s_apart)
                    sp.dma_start(z_scr[taus, :, :].rearrange("a n c -> (a n) c"),
                                 zf[g][:, :, :].rearrange("p h d -> p (h d)")).then_inc(z_stored[g], 16)
            for g in pair:
                for s in (k_stored, y_stored, z_stored):
                    sp.wait_ge(s[g], 16 * NS)

        @block.tensor
        def _(pe):
            pe.wait_ge(s_zeroed, 5)
            with pe.Fori(0, NS) as i:
                t = [i * 2, i * 2 + 1]
                for g in pair:
                    pe.wait_ge(s_hcol, t[g] + 1)
                    b0.wait_free(pe, i, f"ph{g}")
                    pe.transpose(b0.t[:, 0:C], hcol[g][:, :], ident[:, :]).then_inc(b0.full, 1)
                for g in pair:
                    pe.wait_ge(s_yn, t[g] + 1)
                    b1.wait_free(pe, i, f"pn{g}")
                    pe.transpose(b1.t[:, 0:128], yn[g][:, :], ident[:, :]).then_inc(b1.full, 1)
                for g in pair:
                    b1.wait_emptied(pe, i, f"pn{g}")
                    b1.wait_free(pe, i, f"be{g}")
                    pe.matmul(b1.t[:, 0:2 * H], nT[g][:, :], wsT[:, 5 * HD:], start=True, stop=True
                              ).then_inc(b1.full, 1)
                    for b, use, k in ((b2, "q", 0), (b3, "k", 1), (b4, "r", 3), (b5, "v", 2), (b6, "w", 4)):
                        b.wait_free(pe, i, f"{use}{g}")
                        pe.matmul(b.t[:, :], nT[g][:, :], wsT[:, k * HD:(k + 1) * HD], start=True, stop=True
                                  ).then_inc(b.full, 1)
                for g in pair:
                    for k, (b, use) in enumerate(((b2, "Tq"), (b3, "Tk"), (b4, "Tr"))):
                        pe.wait_ge(s_kt, t[g] * 3 + k + 1)
                        b.wait_free(pe, i, f"{use}{g}")
                        for hp in range(4):
                            ins = pe.transpose(b.t[:, hp * 128:(hp + 1) * 128],
                                               kt[g][k][:, 2 * hp:2 * hp + 2, :].rearrange("p h d -> p (h d)"),
                                               ident[:, :])
                        ins.then_inc(b.full, 1)
                    for b, use in ((b2, "Tq"), (b3, "Tk"), (b4, "Tr")):
                        b.wait_emptied(pe, i, f"{use}{g}")
                    for par, b in enumerate((b5, b6)):
                        b.wait_free(pe, i, f"A{g}")
                        apart(pe, s_apart)
                        rows = slice(D * par, D * par + D)
                        for kind in pair:
                            for hp in range(4):
                                for blk in range(4):
                                    wide = 2 * B if blk % 2 == 0 else B
                                    col = (kind * 4 + hp) * 2 * B
                                    ins = pe.matmul(b.t[B * blk:B * blk + B, col:col + wide],
                                                    kT[g][1 + kind][rows, hp, B * blk:B * blk + B],
                                                    kT[g][1 + kind][rows, hp, B * blk:B * blk + wide],
                                                    start=True, stop=True)
                        ins.then_inc(b.full, 1)
                    for par, b in enumerate((b7, b1)):
                        b.wait_free(pe, i, f"P{g}")
                        rows = slice(D * par, D * par + D)
                        for hp in range(4):
                            ins = pe.matmul(b.t[:, hp * 128:(hp + 1) * 128], kT[g][1][rows, hp, :],
                                            kT[g][0][rows, hp, :], start=True, stop=True)
                        ins.then_inc(b.full, 1)
                pe.wait_ge(s_xexp, i * 4 + 4)
                b5.wait_emptied(pe, i, "v1")
                b6.wait_emptied(pe, i, "w1")
                for g in pair:
                    for kind, (b, use) in enumerate(((b2, "ya"), (b3, "yb"))):
                        b.wait_free(pe, i, f"{use}{g}")
                        for h in range(H):
                            ins = pe.matmul(b.t[:, h * D:(h + 1) * D], xexp[:, (g * 2 + kind) * H + h, :],
                                            rhs[g][:, kind * H + h, :], start=True, stop=True)
                        ins.then_inc(b.full, 1)
                for g in pair:
                    for kind, (b, use) in enumerate(((b4, "ca"), (b5, "cb"))):
                        (b2, b3)[kind].wait_emptied(pe, i, f"y{'ab'[kind]}{g}")
                        if kind == 0:
                            b5.wait_emptied(pe, i, f"A{g}")
                            b6.wait_emptied(pe, i, f"A{g}")
                        b.wait_free(pe, i, f"{use}{g}")
                        for h in range(H):
                            ins = pe.matmul(b.t[:, h * D:(h + 1) * D], cexp[g][:, kind * H + h, :],
                                            yi[g][:, kind * H + h, :], start=True, stop=True)
                        ins.then_inc(b.full, 1)
                for g in pair:
                    for kind, (b, use) in enumerate(((b6, "fa"), (b7, "fb"))):
                        (b4, b5)[kind].wait_emptied(pe, i, f"c{'ab'[kind]}{g}")
                        b.wait_free(pe, i, f"{use}{g}")
                        for h in range(H):
                            ins = pe.matmul(b.t[:, h * D:(h + 1) * D], xexp[:, (g * 2 + kind) * H + h, :],
                                            rhs[g][:, kind * H + h, :], start=True, stop=True)
                        ins.then_inc(b.full, 1)
                for g in pair:
                    b6.wait_emptied(pe, i, f"fa{g}")
                    b7.wait_emptied(pe, i, f"P{g}")
                    b1.wait_emptied(pe, i, f"P{g}")
                    b0.wait_free(pe, i, f"z{g}")
                    for h in range(H):
                        ins = pe.matmul(b0.t[:, h * D:(h + 1) * D], pexp[g][:, h, :], yf[g][:, h, :],
                                        start=True, stop=True)
                    ins.then_inc(b0.full, 1)

        @block.scalar
        def _(act):
            with act.Fori(0, NS) as i:
                t = [i * 2, i * 2 + 1]
                PER = 6
                step = Tally(act, s_act, i * PER)
                act.wait_ge(s_zeroed, 5)
                for g in pair:
                    act.activation(hcol[g][:, :].rearrange("c (a n) -> c a n", a=2),
                                   hT[:, :, bass.ds(i * 4 + 2 * g, 2)].rearrange("c n a -> c a n"),
                                   ACT.Copy).then_inc(s_hcol, 1)
                for g in pair:
                    for k, (var, ready) in enumerate(((s_var1, s_rstd1), (s_var2, s_rstd2))):
                        act.wait_ge(var, t[g] + 1)
                        step.link(act.activation(rstd[g][:, 2 + k:3 + k], mv[g][:, 2 * k + 1:2 * k + 2], ACT.Ln, bias=eps))
                        act.activation(rstd[g][:, k:k + 1], rstd[g][:, 2 + k:3 + k], ACT.Exp, scale=-0.5
                                       ).then_inc(ready, 1)
                for g in pair:
                    b1.wait_full(act, i, f"pn{g}")
                    act.activation(nT[g][:, :], b1.t[:, 0:128], ACT.Identity, scale=gam[:, :], bias=bet[:, :]
                                   ).then_inc(b1.free, 1)
                for g in pair:
                    b1.wait_emptied(act, i, f"be{g}")
                    step.link(act.activation(sbeta[g][:, :], bcut[g][:, 0, :], ACT.Exp, scale=-1.0))
                    act.activation(sbeta[g][:, :], sbeta[g][:, :], ACT.Ln, bias=one).then_inc(s_blog, 1)
                    act.wait_ge(s_bsum, t[g] + 1)
                    act.activation(sbeta[g][:, :], sbeta[g][:, :], ACT.Exp, scale=-0.5).then_inc(s_sbeta, 1)
                    for k in range(3):
                        b, use = ((b2, "q"), (b3, "k"), (b4, "r"))[k]
                        b.wait_emptied(act, i, f"{use}{g}")
                        act.activation(ek[k][:, :, :], ek[k][:, :, :], ACT.Exp).then_inc(s_e, 1)
                for g in pair:
                    for k, (b, use) in enumerate(((b2, "Tq"), (b3, "Tk"), (b4, "Tr"))):
                        b.wait_full(act, i, f"{use}{g}")
                        act.activation(kT[g][k][:, :, :].rearrange("p a b -> p (a b)"), b.t[:, :], ACT.Copy
                                       ).then_inc(b.free, 1)
                    for par, b in enumerate((b5, b6)):
                        b.wait_full(act, i, f"A{g}")
                        units = b.t[:, :].rearrange("p (u x) -> p u x", u=8)
                        linv = lin[:, :, :].rearrange("p x (g k v) -> p g v k x", g=2, v=2)
                        act.activation(linv[:, g, par, :, :], units[:, :, 0:B], ACT.Copy)
                        for a in pair:
                            cv = cexp[g][:, :, :].rearrange("p (k v) x -> p v k x", v=2)
                            ins = act.activation(cv[N * a:N * a + B, par, :, N * a + B:N * a + 2 * B],
                                                 units[N * a:N * a + B, :, B:2 * B], ACT.Copy)
                        ins.then_inc(b.free, 1)
                for g in pair:
                    for kind, (b, use) in enumerate(((b2, "ya"), (b3, "yb"))):
                        b.wait_full(act, i, f"{use}{g}")
                        act.activation(yi[g][:, kind * H:(kind + 1) * H, :].rearrange("p h d -> p (h d)"), b.t[:, :],
                                       ACT.Copy).then_inc(b.free, 1)
                for g in pair:
                    for kind, (b, use) in enumerate(((b6, "fa"), (b7, "fb"))):
                        b.wait_full(act, i, f"{use}{g}")
                        if kind == 0:
                            act.wait_ge(y_stored[g], i * 16)
                        act.activation(yf[g][:, kind * H:(kind + 1) * H, :].rearrange("p h d -> p (h d)"), b.t[:, :],
                                       ACT.Copy).then_inc(b.free, 1)
                for g in pair:
                    b0.wait_full(act, i, f"z{g}")
                    act.wait_ge(z_stored[g], i * 16)
                    act.activation(zf[g][:, :, :].rearrange("p h d -> p (h d)"), b0.t[:, :], ACT.Copy
                                   ).then_inc(b0.free, 1)
                assert step.n == PER

        @block.vector
        def _(dve):
            dve.wait_ge(s_zeroed, 5)
            with dve.Fori(0, NS) as i:
                t = [i * 2, i * 2 + 1]
                PER = 2 * 3 + 2 * 6 + 1 + 2 * (B - 1)
                step = Tally(dve, s_dve, i * PER)
                for g in pair:
                    b0.wait_full(dve, i, f"ph{g}")
                    step.link(dve.bn_stats(stats[g][:, :], b0.t[:, 0:C]))
                    apart(dve, s_apart)
                    dve.bn_aggr(mv[g][:, 0:2], stats[g][:, :]).then_inc(s_var1, 1)
                    dve.wait_ge(s_rstd1, t[g] + 1)
                    step.link(dve.tensor_scalar(yln[g][:, :], b0.t[:, 0:C], mv[g][:, 0:1], rstd[g][:, 0:1],
                                                ALU.subtract, ALU.mult))
                    dve.tensor_tensor(res[:, bass.ds(t[g], 1), :].rearrange("p a c -> p (a c)"), b0.t[:, 0:C],
                                      yln[g][:, :], ALU.add).then_inc(b0.free, 1)
                    step.link(dve.bn_stats(stats[g][:, :], yln[g][:, :]))
                    apart(dve, s_apart)
                    dve.bn_aggr(mv[g][:, 2:4], stats[g][:, :]).then_inc(s_var2, 1)
                    dve.wait_ge(s_rstd2, t[g] + 1)
                    dve.tensor_scalar(yn[g][:, :], yln[g][:, :], mv[g][:, 2:3], rstd[g][:, 1:2],
                                      ALU.subtract, ALU.mult).then_inc(s_yn, 1)
                for g in pair:
                    b1.wait_full(dve, i, f"be{g}")
                    step.link(dve.tensor_scalar(bcut[g][:, 0, :], b1.t[:, 0:2 * H], -CUT, None, ALU.max))
                    dve.tensor_tensor(bcut[g][:, 1, :], b1.t[:, 0:2 * H], bcut[g][:, 0, :], ALU.subtract
                                      ).then_inc(b1.free, 1)
                    for k, (b, use) in enumerate(((b2, "q"), (b3, "k"), (b4, "r"))):
                        head = b.t[:, :].rearrange("p (h d) -> p h d", h=H)
                        nm = nmax[:, k * H:(k + 1) * H]
                        b.wait_full(dve, i, f"{use}{g}")
                        step.link(dve.tensor_reduce(nm, head, AX.X, ALU.max, negate=True))
                        dve.wait_ge(s_kt, t[g] * 3)
                        dve.tensor_tensor(ek[k][:, :, :], head, nm[:, :, None].broadcast_to([128, H, D]), ALU.add
                                          ).then_inc(b.free, 1)
                    dve.wait_ge(s_sbeta, t[g] + 1)
                    for kind, (b, use) in enumerate(((b5, "v"), (b6, "w"))):
                        b.wait_full(dve, i, f"{use}{g}")
                        dve.tensor_tensor(rhs[g][:, kind * H:(kind + 1) * H, :],
                                          b.t[:, :].rearrange("p (h d) -> p h d", h=H),
                                          sbeta[g][:, kind * H:(kind + 1) * H, None].broadcast_to([128, H, D]), ALU.mult
                                          ).then_inc(b.free, 1)
                    for k in range(3):
                        dve.wait_ge(s_e, t[g] * 3 + k + 1)
                        ins = dve.tensor_reduce(sums[g][:, k * H:(k + 1) * H], ek[k][:, :, :], AX.X, ALU.add)
                    step.link(ins)
                    step.link(dve.reciprocal(cc[g][:, :], sums[g][:, :]))
                    dve.tensor_tensor(cc[g][:, H:], cc[g][:, H:], sbeta[g][:, :], ALU.mult).then_inc(s_cc, 1)
                for g in pair:
                    for par, b in enumerate((b7, b1)):
                        b.wait_full(dve, i, f"P{g}")
                        dve.tensor_tensor(pexp[g][:, par::2, :], b.t[:, :].rearrange("p (h t) -> p h t", h=4),
                                          maskP[:, None, :].broadcast_to([128, 4, 128]), ALU.mult).then_inc(b.free, 1)
                b5.wait_emptied(dve, i, "A1")
                b6.wait_emptied(dve, i, "A1")
                step.link(dve.transpose(lt[:, :, :], lin[:, :, :]))
                dve.wait_ge(s_xi, i + 1)
                for s in range(B - 1):
                    n, m = B - 1 - s, s + 1
                    low = lt[:, s, s + 1:B]
                    tmp = prod[:, 0:n * m].rearrange("p (r c) -> p r c", c=m)
                    step.link(dve.tensor_tensor(tmp, low[:, :, None].broadcast_to([128, n, m]),
                                                xi[:, s, 0:m][:, None, :].broadcast_to([128, n, m]), ALU.mult))
                    step.link(dve.tensor_tensor(xi[:, s + 1:B, 0:m], xi[:, s + 1:B, 0:m], tmp, ALU.subtract))
                dve.transpose(xT[:, :, :], xi[:, :, :]).then_inc(s_xT, 1)
                for g in pair:
                    for kind, (b, use) in enumerate(((b4, "ca"), (b5, "cb"))):
                        b.wait_full(dve, i, f"{use}{g}")
                        dve.tensor_tensor(rhs[g][:, kind * H:(kind + 1) * H, :],
                                          rhs[g][:, kind * H:(kind + 1) * H, :],
                                          b.t[:, :].rearrange("p (h d) -> p h d", h=H), ALU.subtract
                                          ).then_inc(b.free, 1)
                assert step.n == PER

        @block.gpsimd
        def _(pool):
            for g in pair:
                pool.memset(cexp[g][:, :, :], 0.0).then_inc(s_zeroed, 1)
            pool.memset(xexp[:, :, :], 0.0).then_inc(s_zeroed, 1)
            pool.memset(xid[:, :, :], 0.0).then_inc(s_zeroed, 1)
            pool.wait_ge(s_zeroed, 4)
            pool.memset(xid[:, :, :].rearrange("p a b -> p (a b)")[:, 0::B + 1], 1.0).then_inc(s_zeroed, 1)
            pool.wait_ge(s_zeroed, 5)
            with pool.Fori(0, NS) as i:
                t = [i * 2, i * 2 + 1]
                pool.wait_ge(s_xexp, i * 4)
                pool.wait_ge(s_xT, i)
                apart(pool, s_apart)
                pool.tensor_copy(xi[:, :, :], xid[:, :, :]).then_inc(s_xi, 1)
                for g in pair:
                    pool.wait_ge(s_blog, t[g] + 1)
                    pool.tensor_tensor(sbeta[g][:, :], sbeta[g][:, :], bcut[g][:, 1, :], ALU.subtract).then_inc(s_bsum, 1)
                for g in pair:
                    pool.wait_ge(s_cc, t[g] + 1)
                    pool.wait_ge(k_stored[g], i * 16)
                    for k in range(3):
                        pool.tensor_tensor(kt[g][k][:, :, :], ek[k][:, :, :],
                                           cc[g][:, k * H:(k + 1) * H, None].broadcast_to([128, H, D]), ALU.mult
                                           ).then_inc(s_kt, 1)
                b7.wait_full(pool, i, "P1")
                pool.wait_ge(s_kt, i * 6 + 6)
                pool.wait_ge(s_xT, i + 1)
                apart(pool, s_apart)
                for blk in range(4):
                    rows = slice(B * blk, B * blk + B)
                    pool.tensor_copy(xexp[rows, :, B * blk:B * blk + B],
                                     xT[rows, :, :].rearrange("p t u -> p u t")).then_inc(s_xexp, 1)


def recurrence(nc, k_scr, y_scr, z_scr):
    with ExitStack() as c:
        def sb(name, shape, dt=F32):
            return c.enter_context(nc.sbuf_tensor(name, shape, dt))

        def sem(name):
            return c.enter_context(nc.semaphore(name))
        ks = sb("ks", [TT, N, HP, D])
        ys = sb("ys", [TT, N, HP, D])
        hs = sb("hs", [TT, N, HP, D])
        kp = [sb(f"kp{h}", [TT, N * D]) for h in range(HP)]
        nm = [sb(f"nm{h}", [TT, 1]) for h in range(HP)]
        den = [sb(f"den{h}", [TT, 2]) for h in range(HP)]
        acc = [sb(f"acc{h}", [TT, D]) for h in range(HP)]
        h0 = sb("h0", [TT, D])
        pe_ = [c.enter_context(nc.psum_tensor(f"probs{h}", [128, 512], F32)) for h in range(HP)]
        ps_ = [c.enter_context(nc.psum_tensor(f"coefs{h}", [128, 512], F32)) for h in range(HP)]
        s_in, s_done, s_stored, s_init, s_apart = (sem(s) for s in (
            "pass_loaded", "pass_done", "pass_stored", "h0_set", "waited"))
        s_max, s_exp, s_dve = ([sem(f"{n}{h}") for h in range(HP)] for n in ("max_ready", "exp_ready", "rec_step"))
        block = c.enter_context(nc.Block())
        NPASS = H // HP

        @block.sync
        def _(sp):
            with sp.Fori(0, NPASS) as p:
                cols = bass.ds(p * (HP * D), HP * D)
                sp.wait_ge(s_done, p)
                apart(sp, s_apart)
                sp.wait_ge(s_stored, p * 16)
                apart(sp, s_apart)
                for dst, src in ((ks, k_scr), (ys, y_scr), (hs, z_scr)):
                    sp.dma_start(dst[:, :, :, :].rearrange("p n h d -> p n (h d)"), src[0:TT, :, cols]
                                 ).then_inc(s_in, 16)
                sp.wait_ge(s_done, p + 1)
                apart(sp, s_apart)
                sp.dma_start(z_scr[0:TT, :, cols], hs[:, :, :, :].rearrange("p n h d -> p n (h d)")
                             ).then_inc(s_stored, 16)
            sp.wait_ge(s_stored, 16 * NPASS)

        @block.scalar
        def _(act):
            act.wait_ge(s_init, 1)
            with act.Fori(0, NPASS) as p:
                for t in range(N):
                    for h in range(HP):
                        act.wait_ge(s_max[h], p * N + t + 1)
                        src = hs[:, t - 1, h, :] if t else h0[:, :]
                        act.activation(pe_[h][0:TT, 0:D], src, ACT.Exp, bias=nm[h][:, :],
                                       accum_out=den[h][:, 0:1]).then_inc(s_exp[h], 1)

        @block.vector
        def _(dve):
            dve.memset(h0[:, :], 0.0).then_inc(s_init, 1)
            dve.wait_ge(s_init, 1)
            with dve.Fori(0, NPASS) as p:
                dve.wait_ge(s_in, p * 48 + 48)
                PER = 6 * N
                steps = [Tally(dve, s_dve[h], p * PER) for h in range(HP)]
                for h in range(HP):
                    dve.tensor_reduce(nm[h][:, :], h0[:, :], AX.X, ALU.max, negate=True).then_inc(s_max[h], 1)
                for t in range(N):
                    n = t + 1
                    for h, step in enumerate(steps):
                        dve.wait_ge(s_exp[h], p * N + n)
                        step.link(dve.tensor_tensor(kp[h][:, 0:n * D].rearrange("p (s j) -> p s j", s=n),
                                                    ks[:, 0:n, h, :],
                                                    pe_[h][0:TT, None, 0:D].broadcast_to([TT, n, D]), ALU.mult))
                        step(dve.tensor_reduce(ps_[h][0:TT, 0:n], kp[h][:, 0:n * D].rearrange("p (s j) -> p s j", s=n),
                                               AX.X, ALU.add))
                        step(dve.reciprocal(den[h][:, 1:2], den[h][:, 0:1]))
                    for h, step in enumerate(steps):
                        step.wait()
                        step.link(dve.tensor_tensor(kp[h][:, 0:n * D].rearrange("p (s i) -> p s i", s=n),
                                                    ys[:, 0:n, h, :],
                                                    ps_[h][0:TT, 0:n, None].broadcast_to([TT, n, D]), ALU.mult))
                        step(dve.tensor_reduce(acc[h][:, :], kp[h][:, 0:n * D].rearrange("p (s i) -> p i s", s=n),
                                               AX.X, ALU.add))
                    for h, step in enumerate(steps):
                        step.wait()
                        step.link(dve.scalar_tensor_tensor(out=hs[:, t, h, :], in0=acc[h][:, :],
                                                           scalar=den[h][:, 1:2], in1=hs[:, t, h, :],
                                                           op0=ALU.mult, op1=ALU.add))
                        if n < N:
                            dve.tensor_reduce(nm[h][:, :], hs[:, t, h, :], AX.X, ALU.max, negate=True
                                              ).then_inc(s_max[h], 1)
                dve.memset(h0[:, :], 0.0).then_inc(s_done, 1)
                assert all(s.n == PER for s in steps)


def finish(nc, v):
    ident, identb, ones, woT, wq, wmax, res, eps = (v[k] for k in "ident identb ones woT wq wmax res eps".split())
    z_scr, out = v["z_scr"], v["out"]
    NTT = TT // 2
    with ExitStack() as c:
        def sb(name, shape, dt=F32):
            return c.enter_context(nc.sbuf_tensor(name, shape, dt))

        def sem(name):
            return c.enter_context(nc.semaphore(name))
        LB = 3
        assert NTT % LB == 0
        trio = range(LB)
        rows = [sb(f"hrows{b}", [128, HD]) for b in trio]
        hT = [sb(f"hsT{b}", [128, 4, 128]) for b in trio]
        stats = [sb(f"fstats{b}", [128, 6]) for b in trio]
        mv = [sb(f"fmv{b}", [128, 2]) for b in trio]
        rstd = [sb(f"frstd{b}", [128, 2]) for b in trio]
        big = sb("big", [128, NTT])
        ln = sb("ln", [128, NTT, C])
        amax = sb("amax", [128, 8])
        q = [sb(f"q{b}", [128, 3, C]) for b in trio]
        qb = [sb(f"qb{b}", [128, C], BF16) for b in trio]
        qT = [sb(f"qT{b}", [C, 128], BF16) for b in trio]
        fin = [sb(f"fin{b}", [128, C]) for b in trio]
        pt = [c.enter_context(nc.psum_tensor(f"pt{b}", [128, 512], F32)) for b in trio]
        po = [c.enter_context(nc.psum_tensor(f"po{b}", [128, 512], F32)) for b in trio]
        pg = c.enter_context(nc.psum_tensor("pg", [128, 512], F32))
        s_in = [sem(f"rows_in{b}") for b in trio]
        s_out = [sem(f"stored{b}") for b in trio]
        s_apart, s_t, s_hT, s_o, s_h2, s_var, s_rstd, s_act, s_dve, s_ln, s_a, s_b = (sem(s) for s in (
            "waited rows_turned hsT_ready product_ready h2_ready fvar_ready frstd_ready fact_step fdve_step ln_ready "
            "amax_turned amax_spread").split())
        with nc.Block() as block:
            @block.sync
            def _(sp):
                with sp.Fori(0, NTT // LB) as i:
                    for b in trio:
                        sp.wait_ge(s_t, i * LB)
                        apart(sp, s_apart)
                        sp.dma_start(rows[b][:, :], z_scr[bass.ds(i * (2 * LB) + 2 * b, 2), :, :]
                                     .rearrange("a n c -> (a n) c")).then_inc(s_in[b], 16)

            @block.tensor
            def _(pe):
                with pe.Fori(0, NTT // LB) as i:
                    for b in trio:
                        pe.wait_ge(s_in[b], i * 16 + 16)
                        pe.wait_ge(s_hT, i * LB)
                        for k in range(4):
                            ins = pe.transpose(pt[b][:, k * 128:(k + 1) * 128], rows[b][:, k * 128:(k + 1) * 128],
                                               ident[:, :])
                        ins.then_inc(s_t, 1)
                    for b in trio:
                        pe.wait_ge(s_hT, i * LB + b + 1)
                        pe.wait_ge(s_h2, i * LB)
                        for k in range(4):
                            ins = pe.matmul(po[b][:, 0:C], hT[b][:, k, :], woT[:, k, :], start=(k == 0), stop=(k == 3))
                        ins.then_inc(s_o, 1)

            @block.scalar
            def _(act):
                with act.Fori(0, NTT // LB) as i:
                    for b in trio:
                        act.wait_ge(s_t, i * LB + b + 1)
                        act.wait_ge(s_o, i * LB)
                        act.activation(hT[b][:, :, :].rearrange("p a b -> p (a b)"), pt[b][:, :], ACT.Copy
                                       ).then_inc(s_hT, 1)
                    for b in trio:
                        act.wait_ge(s_var, i * LB + b + 1)
                        act.activation(rstd[b][:, 1:2], mv[b][:, 1:2], ACT.Ln, bias=eps).then_inc(s_act, 1)
                        act.wait_ge(s_act, i * LB + b + 1)
                        act.activation(rstd[b][:, 0:1], rstd[b][:, 1:2], ACT.Exp, scale=-0.5).then_inc(s_rstd, 1)

            @block.vector
            def _(dve):
                with dve.Fori(0, NTT // LB) as i:
                    step = Tally(dve, s_dve, i * LB)
                    for b in trio:
                        h2 = res[:, bass.ds(i * LB + b, 1), :].rearrange("p a c -> p (a c)")
                        dve.wait_ge(s_o, i * LB + b + 1)
                        dve.tensor_tensor(h2, po[b][:, 0:C], h2, ALU.add).then_inc(s_h2, 1)
                        dve.wait_ge(s_h2, i * LB + b + 1)
                        apart(dve, s_apart)
                        step.link(dve.bn_stats(stats[b][:, :], h2))
                        apart(dve, s_apart)
                        dve.bn_aggr(mv[b][:, :], stats[b][:, :]).then_inc(s_var, 1)
                    for b in trio:
                        h2 = res[:, bass.ds(i * LB + b, 1), :].rearrange("p a c -> p (a c)")
                        y = ln[:, bass.ds(i * LB + b, 1), :].rearrange("p a c -> p (a c)")
                        dve.wait_ge(s_rstd, i * LB + b + 1)
                        dve.tensor_scalar(y, h2, mv[b][:, 0:1], rstd[b][:, 0:1], ALU.subtract, ALU.mult
                                          ).then_inc(s_ln, 1)
                        dve.wait_ge(s_ln, i * LB + b + 1)
                        dve.tensor_reduce(big[:, bass.ds(i * LB + b, 1)], y, AX.X, ALU.max, apply_absolute_value=True)
                    assert step.n == LB

        s_qt, s_qT, s_p, s_f, s_e, s_c = (sem(s) for s in (
            "q_turned qT_ready linear_ready fin_ready e_step chain_step").split())
        with nc.Block() as block:
            @block.tensor
            def _(pe):
                pe.wait_ge(s_c, 1)
                pe.transpose(pg[0:1, 0:128], amax[:, 0:1], ident[:, :]).then_inc(s_a, 1)
                pe.wait_ge(s_c, 2)
                pe.matmul(pg[:, 128:129], ones[0:1, :], amax[0:1, 1:2], start=True, stop=True).then_inc(s_b, 1)
                with pe.Fori(0, NTT // LB) as i:
                    for b in trio:
                        pe.wait_ge(s_e, i * (6 * LB) + 6 * (b + 1))
                        pe.wait_ge(s_qT, i * LB)
                        pe.transpose(pt[b][:, 0:64].bitcast(BF16), qb[b][:, :], identb[:, :]).then_inc(s_qt, 1)
                    for b in trio:
                        pe.wait_ge(s_qT, i * LB + b + 1)
                        pe.wait_ge(s_f, i * LB)
                        pe.matmul(po[b][:, 0:C], qT[b][:, :], wq[:, :], start=True, stop=True).then_inc(s_p, 1)

            @block.scalar
            def _(act):
                with act.Fori(0, NTT // LB) as i:
                    for b in trio:
                        act.wait_ge(s_qt, i * LB + b + 1)
                        act.wait_ge(s_p, i * LB)
                        act.activation(qT[b][:, :], pt[b][:, 0:64].bitcast(BF16), ACT.Copy).then_inc(s_qT, 1)

            @block.vector
            def _(dve):
                step = Tally(dve, s_c)
                step(dve.tensor_reduce(amax[:, 0:1], big[:, :], AX.X, ALU.max))
                dve.wait_ge(s_a, 1)
                step(dve.tensor_reduce(amax[0:1, 1:2], pg[0:1, 0:128], AX.X, ALU.max))
                dve.wait_ge(s_b, 1)
                step.link(dve.tensor_scalar(amax[:, 2:3], pg[:, 128:129], 1e-12, None, ALU.max))
                step.link(dve.reciprocal(amax[:, 3:4], amax[:, 2:3]))
                step.link(dve.tensor_scalar(amax[:, 3:4], amax[:, 3:4], FP8_MAX, None, ALU.mult))
                step.link(dve.tensor_scalar(amax[:, 4:5], amax[:, 2:3], 1.0 / FP8_MAX, None, ALU.mult))
                step.link(dve.tensor_scalar(amax[:, 5:6], wmax[:, :], 1.0 / FP8_MAX, None, ALU.mult))
                step.link(dve.tensor_tensor(amax[:, 6:7], amax[:, 4:5], amax[:, 5:6], ALU.mult))
                with dve.Fori(0, NTT // LB) as i:
                    step = Tally(dve, s_e, i * (6 * LB))
                    for b in trio:
                        y = ln[:, bass.ds(i * LB + b, 1), :].rearrange("p a c -> p (a c)")
                        quantise(dve, step, qb[b][:, :], y, amax[:, 3:4], q[b])
                    for b in trio:
                        h2 = res[:, bass.ds(i * LB + b, 1), :].rearrange("p a c -> p (a c)")
                        dve.wait_ge(s_p, i * LB + b + 1)
                        dve.wait_ge(s_out[b], i * 32)
                        dve.scalar_tensor_tensor(out=fin[b][:, :], in0=po[b][:, 0:C], scalar=amax[:, 6:7], in1=h2,
                                                 op0=ALU.mult, op1=ALU.add).then_inc(s_f, 1)
                    assert step.n == 6 * LB

            @block.sync
            def _(sp):
                with sp.Fori(0, NTT // LB) as i:
                    for b in trio:
                        sp.wait_ge(s_f, i * LB + b + 1)
                        apart(sp, s_apart)
                        for a in range(2):
                            sp.dma_start(out[:, bass.ds(i * (2 * LB) + 2 * b + a, 1), :].rearrange("n a c -> (a n) c"),
                                         fin[b][N * a:N * a + N, :]).then_inc(s_out[b], 16)
                for b in trio:
                    sp.wait_ge(s_out[b], 32 * (NTT // LB))


_INS = ["x", "L0_tok_Wf", "L0_tok_bf", "L0_tok_Wi", "L0_tok_bi", "L0_tok_Wh", "L0_tok_bh", "L0_attn_W_slow",
        "L0_attn_W_out", "L0_attn_ln_gamma", "L0_attn_ln_beta", "L0_ffn_weight"]


def kernel(**inputs):
    import numpy as np
    import concourse.bacc as bacc
    from concourse.bass_utils import run_bass_kernel_spmd

    nc = bacc.Bacc("TRN2", target_bir_lowering=False, num_devices=1)
    arrays, args = {}, []
    for name in _INS:
        a = np.ascontiguousarray(inputs[name])
        arrays[f"in_{name}"] = a
        args.append(nc.dram_tensor(f"in_{name}", a.shape, mybir.dt.from_np(a.dtype), kind="ExternalInput").ap())
    out = nc.dram_tensor("out", (N, TT, C), F32, kind="ExternalOutput").ap()
    audio_layer(nc, *args, out)
    return run_bass_kernel_spmd(nc, [arrays], core_ids=[0]).results[0]["out"]
```

```python
import concourse.bass as bass
from concourse import mybir
from contextlib import ExitStack

F32 = mybir.dt.float32
BF16 = mybir.dt.bfloat16
U32 = mybir.dt.uint32
ALU = mybir.AluOpType
ACT = mybir.ActivationFunctionType
AX = mybir.AxisListType

N = 64
T = 125
TT = T + 1
TP = 128
C = 128
H, D = 8, 64
HD = H * D
PR = 5 * D + 2
NT = TP // 2
NS = NT // 2
EPS = 1e-5
CUT = 40.0
FP8_MAX = 448.0
HP = 4


class Tally:

    def __init__(self, eng, sem, start=0):
        self.eng, self.sem, self.n, self.start = eng, sem, 0, start

    def __call__(self, ins):
        ins.then_inc(self.sem, 1)
        self.n += 1

    def wait_for(self, n):
        self.eng.wait_ge(self.sem, self.start + n)

    def wait(self):
        self.wait_for(self.n)

    def link(self, ins):
        self(ins)
        self.wait()


def apart(eng, sem):
    eng.sem_inc(sem, 1)


def audio_layer(nc, x, Wf, bf, Wi, bi, Wh, bh, W_slow, W_out, gamma, beta, weight, out):
    k_scr = nc.dram_tensor("k_scr", (TP, N, HD), F32, kind="Internal").ap()
    y_scr = nc.dram_tensor("y_scr", (TP, N, HD), F32, kind="Internal").ap()
    z_scr = nc.dram_tensor("z_scr", (TP, N, HD), F32, kind="Internal").ap()
    res_scr = nc.dram_tensor("res_scr", (TP, N, C), F32, kind="Internal").ap()

    ctx = ExitStack()
    with ctx:
        def keep(name, shape, dt=F32):
            return ctx.enter_context(nc.sbuf_tensor(name, shape, dt))

        ident = keep("ident", [128, 128])
        identb = keep("identb", [128, 128], BF16)
        ones = keep("ones", [128, 128])
        consts = keep("consts", [128, 4])
        zero, one, eps, bhh = (consts[:, k:k + 1] for k in range(4))
        woT = keep("woT", [C, 4, C])
        wq = keep("wq", [C, C], BF16)
        wmax = keep("wmax", [128, 1])
        build_weights_and_mid(nc, locals())
        recurrence(nc, k_scr, y_scr, z_scr, ident)
        finish(nc, locals())


def build_weights_and_mid(nc, v):
    with ExitStack() as c:
        def sb(name, shape, dt=F32):
            return c.enter_context(nc.sbuf_tensor(name, shape, dt))
        wsT = sb("wsT", [C, 5 * HD + 2 * H])
        gates = sb("gates", [C, 3, C])
        biases = sb("biases", [C, 8])
        gam, bet = sb("gam", [C, 1]), sb("bet", [C, 1])
        hT = sb("hT", [C, N, TP])
        mask = sb("mask", [128, N])
        weights(nc, v, wsT, gates, biases, gam, bet, hT, mask)
        mingru(nc, v, gates, biases, hT)
        attention_setup(nc, v, wsT, gam, bet, hT, mask)


def weights(nc, v, wsT, gates, biases, gam, bet, hT, mask):
    ident, identb, ones, consts, woT, wq, wmax = (v[k] for k in "ident identb ones consts woT wq wmax".split())
    W_slow, W_out = v["W_slow"], v["W_out"]
    with ExitStack() as c:
        def sb(name, shape, dt=F32):
            return c.enter_context(nc.sbuf_tensor(name, shape, dt))

        def sem(name):
            return c.enter_context(nc.semaphore(name))
        maskP = sb("maskP", [128, 128])
        rows = sb("rows", [128, 5, 4, C])
        brows = sb("brows", [2 * H, C])
        worows = sb("worows", [C, HD])
        w8 = sb("w8", [C, C])
        q8 = sb("q8", [C, 3, C])
        st = sb("st", [128, 8])
        banks = [c.enter_context(nc.psum_tensor(f"turn{k}", [128, 512], F32)) for k in range(8)]
        loaded, consts_set, turned, copied, chain = (sem(s) for s in (
            "loaded", "consts_set", "turned", "copied", "w8_step"))
        amax_t, amax_b = sem("amax_turned"), sem("amax_spread")
        per_head = W_slow.rearrange("(h r) c -> h r c", r=PR)
        block = c.enter_context(nc.Block())
        NLOAD = 10 + 2 + 1 + 1 + 3 + 3 + 2

        @block.sync
        def _(sp):
            for kind in range(5):
                for par in range(2):
                    sp.dma_start(rows[D * par:D * par + D, kind, :, :],
                                 per_head[par::2, kind * D:(kind + 1) * D, :].rearrange("h d c -> d h c")
                                 ).then_inc(loaded, 16)
            for r in range(2):
                sp.dma_start(brows[H * r:H * r + H, :], per_head[:, 5 * D + r, :]).then_inc(loaded, 16)
            sp.dma_start(worows[:, :], W_out).then_inc(loaded, 16)
            sp.dma_start(w8[:, :], v["weight"]).then_inc(loaded, 16)
            for k, name in enumerate(("Wf", "Wi", "Wh")):
                sp.dma_start(gates[:, k, :], v[name]).then_inc(loaded, 16)
            for k, name in enumerate(("bf", "bi", "bh")):
                sp.dma_start(biases[:, k:k + 1], v[name].rearrange("(p a) -> p a", a=1)).then_inc(loaded, 16)
            sp.dma_start(gam[:, :], v["gamma"].rearrange("(p a) -> p a", a=1)).then_inc(loaded, 16)
            sp.dma_start(bet[:, :], v["beta"].rearrange("(p a) -> p a", a=1)).then_inc(loaded, 16)

        @block.gpsimd
        def _(pool):
            step = Tally(pool, consts_set)
            step(pool.memset(ident[:, :], 0.0))
            step(pool.memset(maskP[:, :], 1.0))
            step(pool.memset(ones[:, :], 1.0))
            step(pool.memset(consts[:, 0:1], 0.0))
            step(pool.memset(consts[:, 1:2], 1.0))
            step(pool.memset(consts[:, 2:3], EPS))
            step(pool.memset(hT[:, :, :], 0.0))
            step.wait()
            step.link(pool.affine_select(out=ident[:, :], in_=ident[:, :], compare_op=ALU.not_equal, fill=1.0,
                                         base=0, pattern=[[-1, 128]], channel_multiplier=1))
            step.link(pool.affine_select(out=maskP[:, :], in_=maskP[:, :], compare_op=ALU.is_ge, fill=0.0,
                                         base=0, pattern=[[1, 128]], channel_multiplier=-1))
            step.link(pool.affine_select(out=maskP[:, N:], in_=maskP[:, N:], compare_op=ALU.is_ge, fill=0.0,
                                         base=-N, pattern=[[0, N]], channel_multiplier=1))
            step.link(pool.tensor_tensor(mask[:, :], maskP[:, 0:N], maskP[:, N:], ALU.add))

        @block.tensor
        def _(pe):
            pe.wait_ge(loaded, 16 * NLOAD)
            pe.wait_ge(consts_set, 11)
            for kind in range(5):
                for hp in range(4):
                    ins = pe.transpose(banks[kind][:, hp * 128:(hp + 1) * 128], rows[:, kind, hp, :], ident[:, :])
            pe.transpose(banks[5][:, 0:2 * H], brows[:, :], ident[0:2 * H, 0:2 * H])
            for k in range(4):
                ins = pe.transpose(banks[6][:, k * 128:(k + 1) * 128], worows[:, k * 128:(k + 1) * 128], ident[:, :])
            ins.then_inc(turned, 1)
            pe.wait_ge(chain, 1)
            pe.transpose(banks[7][0:1, 0:128], st[:, 0:1], ident[:, :]).then_inc(amax_t, 1)
            pe.wait_ge(chain, 2)
            pe.matmul(banks[7][:, 128:129], ones[0:1, :], st[0:1, 1:2], start=True, stop=True).then_inc(amax_b, 1)

        @block.scalar
        def _(act):
            act.preload_act_table_set("natural_log_exp_and_others")
            act.wait_ge(turned, 1)
            for kind in range(5):
                act.activation(wsT[:, kind * HD:(kind + 1) * HD], banks[kind][:, :], ACT.Copy)
            act.activation(wsT[:, 5 * HD:], banks[5][:, 0:2 * H], ACT.Copy)
            act.activation(woT[:, :, :].rearrange("p a b -> p (a b)"), banks[6][:, :], ACT.Copy).then_inc(copied, 1)
            act.wait_ge(copied, 1)

        @block.vector
        def _(dve):
            step = Tally(dve, chain)
            dve.wait_ge(loaded, 16 * NLOAD)
            step(dve.tensor_reduce(st[:, 0:1], w8[:, :], AX.X, ALU.max, apply_absolute_value=True))
            dve.wait_ge(amax_t, 1)
            step(dve.tensor_reduce(st[0:1, 1:2], banks[7][0:1, 0:128], AX.X, ALU.max))
            dve.wait_ge(amax_b, 1)
            step.link(dve.tensor_scalar(wmax[:, :], banks[7][:, 128:129], 1e-12, None, ALU.max))
            step.link(dve.reciprocal(st[:, 2:3], wmax[:, :]))
            step.link(dve.tensor_scalar(st[:, 3:4], st[:, 2:3], FP8_MAX, None, ALU.mult))
            quantise(dve, step, wq[:, :], w8[:, :], st[:, 3:4], q8)
            dve.wait_ge(consts_set, 11)
            step.link(dve.tensor_scalar(biases[:, 3:6], biases[:, 0:3], -1.0, None, ALU.mult))
            step.link(dve.tensor_scalar(consts[:, 3:4], biases[:, 2:3], 0.5, None, ALU.add))
            step.link(dve.tensor_copy(identb[:, :], ident[:, :]))


def newton(dve, step, r, var, tmp):
    step.link(dve.tensor_scalar(tmp[:, 0:1], var, EPS, -0.5, ALU.add, ALU.mult))
    step.link(dve.tensor_scalar(tmp[:, 1:2], r, r, tmp[:, 0:1], ALU.mult, ALU.mult))
    step.link(dve.tensor_scalar(tmp[:, 1:2], tmp[:, 1:2], 1.5, None, ALU.add))
    step.link(dve.tensor_tensor(r, r, tmp[:, 1:2], ALU.mult))


def quantise(dve, step, to, src, scale, q):
    step.link(dve.tensor_scalar(q[:, 0, :], src, scale, FP8_MAX, ALU.mult, ALU.min))
    step.link(dve.tensor_scalar(q[:, 0, :], q[:, 0, :], -FP8_MAX, None, ALU.max))
    step.link(dve.tensor_scalar(q[:, 1, :].bitcast(U32), q[:, 0, :].bitcast(U32), 0x7F800000, None, ALU.bitwise_and))
    step.link(dve.tensor_scalar(q[:, 1, :], q[:, 1, :], 2.0 ** -6, 1.5 * 2.0 ** 20, ALU.max, ALU.mult))
    step.link(dve.tensor_tensor(q[:, 2, :], q[:, 0, :], q[:, 1, :], ALU.add))
    step.link(dve.tensor_tensor(to, q[:, 2, :], q[:, 1, :], ALU.subtract))



def mingru(nc, v, gates, biases, hT):
    ident, one, bhh = v["ident"], v["one"], v["bhh"]
    G = 4
    NG = N // G
    W = G * T
    nbh = biases[:, 5:6]

    def steps(row):
        return row.rearrange("p (g t) -> p g t", g=G)

    with ExitStack() as c:
        def sb(name, shape, dt=F32):
            return c.enter_context(nc.sbuf_tensor(name, shape, dt))

        def sem(name):
            return c.enter_context(nc.semaphore(name))

        def pb(name):
            return c.enter_context(nc.psum_tensor(name, [128, 512], F32))
        xin = [sb(f"xin{b}", [T, G, C]) for b in range(2)]
        xT = [sb(f"xT{b}", [C, W]) for b in range(2)]
        px = [pb(f"px{b}") for b in range(2)]
        pz = [[pb(f"pz{b}{k}") for k in range(3)] for b in range(2)]
        zc = [sb(f"zc{b}", [C, 2, W]) for b in range(2)]
        zr = [sb(f"zr{b}", [C, 2, W]) for b in range(2)]
        ex = [sb(f"ex{b}", [C, 2, W]) for b in range(2)]
        sp_ = [sb(f"softp{b}", [C, 2, W]) for b in range(2)]
        df = [sb(f"diff{b}", [C, W]) for b in range(2)]
        dc = [sb(f"diffc{b}", [C, W]) for b in range(2)]
        ld = [sb(f"ld{b}", [C, W]) for b in range(2)]
        rr = [sb(f"beyond{b}", [C, G, TT]) for b in range(2)]
        inv = [sb(f"invf{b}", [C, G, TT]) for b in range(2)]
        fg = [sb(f"fgate{b}", [C, W]) for b in range(2)]
        la = [sb(f"la{b}", [C, 3, W]) for b in range(2)]
        eh = [sb(f"eh{b}", [C, W]) for b in range(2)]
        sg = [sb(f"sg{b}", [C, W]) for b in range(2)]
        aa = [sb(f"aa{b}", [C, G, TT]) for b in range(2)]
        bb = [sb(f"bb{b}", [C, G, TT]) for b in range(2)]
        x_in = [sem(f"x_in{b}") for b in range(2)]
        x_turned, x_copied, z_made, act_step, dve_step, pool_step, edge, s_apart = (sem(s) for s in (
            "x_turned", "x_copied", "z_made", "gru_act", "gru_dve", "gru_pool", "edges", "waited"))
        AS, DS, PS = 5, 13, 6
        block = c.enter_context(nc.Block())

        @block.sync
        def _(sp):
            with sp.Fori(0, NG // 2) as i:
                for b in range(2):
                    sp.wait_ge(x_turned, i * 2 + 1)
                    apart(sp, s_apart)
                    sp.dma_start(xin[b][:, :, :], v["x"][bass.ds(i * (2 * G) + b * G, G), :, :]
                                 .rearrange("g t c -> t g c")).then_inc(x_in[b], 16)

        @block.tensor
        def _(pe):
            for s, n in ((x_turned, 1), (x_copied, 1), (z_made, 1), (act_step, AS + 1), (dve_step, DS + 1),
                         (pool_step, PS + 1)):
                pe.sem_inc(s, n)
            with pe.Fori(0, NG // 2) as i:
                for b in range(2):
                    g = i * 2 + b
                    pe.wait_ge(x_in[b], i * 16 + 16)
                    pe.wait_ge(x_copied, g + 1)
                    for k in range(G):
                        ins = pe.transpose(px[b][:, k * T:(k + 1) * T], xin[b][:, k, :], ident[0:T, 0:T])
                    ins.then_inc(x_turned, 1)
                    pe.wait_ge(x_copied, g + 1 + 1)
                    pe.wait_ge(act_step, g * AS + 1)
                    pe.wait_ge(dve_step, g * DS + 1)
                    for k in range(3):
                        ins = pe.matmul(pz[b][k][:, 0:W], gates[:, k, :], xT[b][:, :], start=True, stop=True)
                    ins.then_inc(z_made, 1)

        @block.scalar
        def _(act):
            act.preload_act_table_set("natural_log_exp_and_others")

            def turn(g, b):
                act.wait_ge(x_turned, g + 2)
                if not isinstance(g, int) or g > 0:
                    act.wait_ge(z_made, g)
                act.activation(xT[b][:, :], px[b][:, 0:W], ACT.Copy).then_inc(x_copied, 1)

            def group(g, b, more):
                a0, d0, p0 = (g + 1) * AS + 1, (g + 1) * DS + 1, (g + 1) * PS + 1
                act.wait_ge(z_made, g + 2)
                act.wait_ge(pool_step, g * PS + 1)
                act.activation(eh[b][:, :], pz[b][2][:, 0:W], ACT.Exp, bias=nbh, scale=-1.0).then_inc(act_step, 1)
                act.wait_ge(dve_step, d0 + 2)
                act.activation(ex[b][:, :, :], zc[b][:, :, :], ACT.Exp, scale=-1.0).then_inc(act_step, 1)
                act.wait_ge(act_step, a0 + 2)
                act.activation(sp_[b][:, :, :], ex[b][:, :, :], ACT.Ln, bias=one).then_inc(act_step, 1)
                if more:
                    turn(g + 1, 1 - b)
                act.wait_ge(dve_step, d0 + 5)
                act.activation(ld[b][:, :], dc[b][:, :], ACT.Exp).then_inc(act_step, 1)
                act.wait_ge(pool_step, p0 + 4)
                act.activation(la[b][:, 1, :], la[b][:, 1, :], ACT.Exp).then_inc(act_step, 1)
            turn(0, 0)
            with act.Fori(0, NG // 2 - 1) as i:
                for b in range(2):
                    group(i * 2 + b, b, True)
            group(NG - 2, 0, True)
            group(NG - 1, 1, False)

        @block.vector
        def _(dve):
            for b in range(2):
                dve.memset(aa[b][:, :, 0:1], 0.0)
                dve.memset(bb[b][:, :, 0:1], 0.5)
                dve.memset(rr[b][:, :, 0:1], 0.0)
                dve.memset(inv[b][:, :, 0:1], 1.0).then_inc(edge, 1)
            dve.wait_ge(edge, 2)
            with dve.Fori(0, NG // 2) as i:
                for b in range(2):
                    g = i * 2 + b
                    a0, d0, p0 = (g + 1) * AS + 1, (g + 1) * DS + 1, (g + 1) * PS + 1
                    dve.wait_ge(z_made, g + 2)
                    dve.wait_ge(pool_step, g * PS + 1)
                    for k in range(2):
                        dve.tensor_scalar(zc[b][:, k, :], pz[b][k][:, 0:W], biases[:, k:k + 1], -CUT,
                                          ALU.add, ALU.max).then_inc(dve_step, 1)
                    for k in range(2):
                        dve.wait_ge(dve_step, d0 + 1 + k)
                        dve.scalar_tensor_tensor(out=zr[b][:, k, :], in0=pz[b][k][:, 0:W], scalar=biases[:, k:k + 1],
                                                 in1=zc[b][:, k, :], op0=ALU.add, op1=ALU.subtract
                                                 ).then_inc(dve_step, 1)
                    dve.wait_ge(pool_step, p0 + 2)
                    dve.tensor_scalar(dc[b][:, :], df[b][:, :], CUT, None, ALU.min).then_inc(dve_step, 1)
                    dve.wait_ge(act_step, a0 + 1)
                    dve.tensor_scalar(eh[b][:, :], eh[b][:, :], 1.0, None, ALU.add).then_inc(dve_step, 1)
                    dve.wait_ge(dve_step, d0 + 6)
                    dve.reciprocal(sg[b][:, :], eh[b][:, :]).then_inc(dve_step, 1)
                    dve.wait_ge(dve_step, d0 + 7)
                    dve.scalar_tensor_tensor(out=sg[b][:, :], in0=pz[b][2][:, 0:W], scalar=bhh,
                                             in1=sg[b][:, :], op0=ALU.add, op1=ALU.max).then_inc(dve_step, 1)
                    dve.wait_ge(act_step, a0 + 4)
                    dve.tensor_scalar(inv[b][:, :, 1:TT], steps(ld[b][:, :]), 1.0, None, ALU.add).then_inc(dve_step, 1)
                    dve.wait_ge(dve_step, d0 + 9)
                    dve.reciprocal(steps(fg[b][:, :]), inv[b][:, :, 1:TT]).then_inc(dve_step, 1)
                    dve.wait_ge(pool_step, p0 + 6)
                    dve.wait_ge(act_step, a0 + 5)
                    dve.tensor_tensor(bb[b][:, :, 1:TT], steps(la[b][:, 0, :]), steps(sg[b][:, :]), ALU.mult
                                      ).then_inc(dve_step, 1)
                    dve.tensor_tensor(aa[b][:, :, 1:TT], steps(la[b][:, 1, :]), steps(la[b][:, 2, :]), ALU.mult
                                      ).then_inc(dve_step, 1)
                    dve.wait_ge(dve_step, d0 + 12)
                    for s in range(G):
                        ins = dve.tensor_tensor_scan(hT[:, bass.ds(g * G + s, 1), 0:TT].rearrange("p a t -> p (a t)"),
                                                     aa[b][:, s, :], bb[b][:, s, :], 0.0, ALU.mult, ALU.add)
                    ins.then_inc(dve_step, 1)

        @block.gpsimd
        def _(pool):
            pool.wait_ge(edge, 2)
            with pool.Fori(0, NG // 2) as i:
                for b in range(2):
                    g = i * 2 + b
                    a0, d0, p0 = (g + 1) * AS + 1, (g + 1) * DS + 1, (g + 1) * PS + 1
                    pool.wait_ge(act_step, a0 + 3)
                    pool.wait_ge(dve_step, d0 + 4)
                    pool.tensor_tensor(sp_[b][:, :, :], sp_[b][:, :, :], zr[b][:, :, :], ALU.subtract).then_inc(pool_step, 1)
                    pool.wait_ge(pool_step, p0 + 1)
                    pool.tensor_tensor(df[b][:, :], sp_[b][:, 0, :], sp_[b][:, 1, :], ALU.subtract).then_inc(pool_step, 1)
                    pool.wait_ge(dve_step, d0 + 5)
                    pool.tensor_tensor(rr[b][:, :, 1:TT], steps(df[b][:, :]), steps(dc[b][:, :]), ALU.subtract
                                       ).then_inc(pool_step, 1)
                    pool.wait_ge(pool_step, p0 + 3)
                    pool.tensor_tensor(steps(la[b][:, 1, :]), rr[b][:, :, 0:T], rr[b][:, :, 1:TT], ALU.subtract
                                       ).then_inc(pool_step, 1)
                    pool.wait_ge(dve_step, d0 + 10)
                    pool.tensor_tensor(steps(la[b][:, 2, :]), inv[b][:, :, 0:T], steps(fg[b][:, :]), ALU.mult
                                       ).then_inc(pool_step, 1)
                    pool.tensor_tensor(la[b][:, 0, :], ld[b][:, :], fg[b][:, :], ALU.mult).then_inc(pool_step, 1)


class Bank:

    def __init__(self, tensor, full, free, uses):
        self.t, self.full, self.free = tensor, full, free
        self.uses = [(u.split("-")[0], int((u.split("-") + [0])[1])) for u in uses.split()]

    def before(self, i):
        if isinstance(i, int):
            return sum(min(max(i - lag, 0), NS) for _, lag in self.uses)
        return i * len(self.uses) - sum(lag for _, lag in self.uses)

    def index(self, i, use):
        present = [u for u, lag in self.uses if not isinstance(i, int) or 0 <= i - lag < NS]
        return self.before(i) + present.index(use)

    def wait_free(self, pe, i, use):
        pe.wait_ge(self.free, self.index(i, use) + 1)

    def wait_emptied(self, eng, i, use):
        eng.wait_ge(self.free, self.index(i, use) + 2)

    def wait_full(self, eng, i, use):
        eng.wait_ge(self.full, self.index(i, use) + 1)


def pipeline(eng, step):
    step(0, 0, (True, False, False))
    step(1, 1, (True, True, False))
    with eng.Fori(0, NS // 2 - 1) as j:
        for par in range(2):
            step(j * 2 + 2 + par, par, (True, True, True))
    step(NS, 0, (False, True, True))
    step(NS + 1, 1, (False, False, True))


def attention_setup(nc, v, wsT, gam, bet, hT, mask):
    ident, one, eps = v["ident"], v["one"], v["eps"]
    k_scr, y_scr, z_scr = v["k_scr"], v["y_scr"], v["z_scr"]
    B = 32
    U = 2 * 2 * H
    with ExitStack() as c:
        def sb(name, shape, dt=F32):
            return c.enter_context(nc.sbuf_tensor(name, shape, dt))

        def sem(name):
            return c.enter_context(nc.semaphore(name))

        def bank(k, uses):
            return Bank(c.enter_context(nc.psum_tensor(f"bank{k}", [128, 512], F32)),
                        sem(f"full{k}"), sem(f"free{k}"), uses)
        pair = range(2)
        hcol = [sb(f"hcol{g}", [C, 128]) for g in pair]
        stats = [sb(f"stats{g}", [128, 6]) for g in pair]
        mv = [sb(f"mv{g}", [128, 4]) for g in pair]
        rstd = [sb(f"rstd{g}", [128, 4]) for g in pair]
        yln = [sb(f"yln{g}", [128, C]) for g in pair]
        yn = [sb(f"yn{g}", [128, C]) for g in pair]
        res = [sb(f"res{g}", [128, C]) for g in pair]
        r_stored = [sem(f"r_stored{g}") for g in pair]
        nT = [sb(f"nT{g}", [C, 128]) for g in pair]
        sbeta = [sb(f"sbeta{g}", [128, 2 * H]) for g in pair]
        bcut = [sb(f"bcut{g}", [128, 2, 2 * H]) for g in pair]
        nmax = sb("nmax", [128, 3 * H])
        ek = [[sb(f"ek{g}{k}", [128, H, D]) for k in range(3)] for g in pair]
        sums = [sb(f"sums{g}", [128, 3 * H]) for g in pair]
        cc = [sb(f"cc{g}", [128, 3 * H]) for g in pair]
        kt = [[sb(f"kt{g}{k}", [128, H, D]) for k in range(3)] for g in pair]
        kT = [[sb(f"kT{g}{k}", [128, 4, 128]) for k in range(3)] for g in pair]
        lin = sb("lin", [128, B, U])
        lt = sb("lt", [128, B, B])
        xi = sb("xi", [128, B, B])
        prod = sb("prod", [128, 2, B * B // 4])
        xid = sb("xid", [128, B, B])
        xT = sb("xT", [128, B, U])
        xexp = sb("xexp", [128, U, N])
        yi = [sb(f"yi{g}", [128, 2 * H, D]) for g in pair]
        yf = [sb(f"yf{g}", [128, 2 * H, D]) for g in pair]
        zf = [sb(f"zf{g}", [128, H, D]) for g in pair]
        rhs = [[sb(f"rhs{r}{g}", [128, 2 * H, D]) for g in pair] for r in pair]
        cexp = [[sb(f"cexp{r}{g}", [128, 2 * H, N]) for g in pair] for r in pair]
        pexp = [[sb(f"pexp{r}{g}", [128, H, N]) for g in pair] for r in pair]
        b0 = bank(0, "ph pn1")
        b1 = bank(1, "yb1-1 be0 be1 P")
        b2 = bank(2, "ya0-1 q0 q1 Tq0 Tq1 ca1-1")
        b3 = bank(3, "yb0-1 k0 k1 Tk0 Tk1 cb1-1")
        b4 = bank(4, "z0-2 r0 r1 Tr0 Tr1 ca0-1")
        b5 = bank(5, "ya1-1 v0 v1 A0 A1 cb0-1")
        b6 = bank(6, "fa0-2 fa1-2 z1-2 w0 w1 A0 A1")
        b7 = bank(7, "fb0-2 fb1-2 pn0 P")
        bn, bz = (b7, b0), (b4, b6)
        by, bc = ((b2, b3), (b5, b1)), ((b4, b5), (b2, b3))
        (s_hcol, s_var1, s_rstd1, s_var2, s_rstd2, s_yn, s_blog, s_bsum, s_sbeta, s_e, s_cc, s_kt, s_xT, s_xact,
         s_xpool, s_xi, s_apart, s_zeroed, s_dve, s_act) = (sem(s) for s in (
            "hcol_ready var1_ready rstd1_ready var2_ready rstd2_ready yn_ready beta_log beta_softplus sbeta_ready e_ready "
            "scales_ready kt_ready xT_ready xexp_act xexp_pool xi_reset waited zeroed dve_step act_step").split())
        k_stored = [sem(f"k_stored{g}") for g in pair]
        y_stored = [sem(f"y_stored{g}") for g in pair]
        z_stored = [sem(f"z_stored{g}") for g in pair]
        block = c.enter_context(nc.Block())

        def per_tau(pe, out, lhsT, rhs_):
            for a in pair:
                rows = slice(N * a, N * a + N)
                ins = pe.matmul(out[rows, :], lhsT[rows, :], rhs_[rows, :], start=True, stop=True)
            return ins

        @block.sync
        def _(sp):
            def rows_of(scr, i, g):
                return scr[bass.ds(i * 4 + 2 * g, 2), :, :].rearrange("a n c -> (a n) c")

            def step(i, par, live):
                if live[2]:
                    for g in pair:
                        b7.wait_emptied(sp, i, f"fb{g}")
                        apart(sp, s_apart)
                        sp.dma_start(rows_of(y_scr, i - 2, g), yf[g][:, H:, :].rearrange("p h d -> p (h d)")
                                     ).then_inc(y_stored[g], 16)
                if live[0]:
                    b0.wait_emptied(sp, i, "ph")
                    apart(sp, s_apart)
                    for g in pair:
                        sp.dma_start(rows_of(v["res_scr"], i, g), res[g][:, :]).then_inc(r_stored[g], 16)
                if live[2]:
                    for g in pair:
                        bz[g].wait_emptied(sp, i, f"z{g}")
                        apart(sp, s_apart)
                        sp.dma_start(rows_of(z_scr, i - 2, g), zf[g][:, :, :].rearrange("p h d -> p (h d)")
                                     ).then_inc(z_stored[g], 16)
                if live[0]:
                    for g in pair:
                        sp.wait_ge(s_kt, (i * 2 + g) * 3 + 3 + 1)
                        apart(sp, s_apart)
                        sp.dma_start(rows_of(k_scr, i, g), kt[g][2][:, :, :].rearrange("p h d -> p (h d)")
                                     ).then_inc(k_stored[g], 16)
            pipeline(sp, step)
            for g in pair:
                for s in (r_stored, k_stored, y_stored, z_stored):
                    sp.wait_ge(s[g], 16 * NS + 1)

        @block.tensor
        def _(pe):
            for s in (*(b.free for b in (b0, b1, b2, b3, b4, b5, b6, b7)), *k_stored, *y_stored, *z_stored,
                      *r_stored, s_kt, s_xact, s_xpool, s_xT):
                pe.sem_inc(s, 1)
            pe.wait_ge(s_zeroed, 7)

            def step(i, par, live):
                if live[0]:
                    pe.wait_ge(s_hcol, i + 1)
                    b0.wait_free(pe, i, "ph")
                    for g in pair:
                        ins = pe.transpose(b0.t[:, g * 128:g * 128 + C], hcol[g][:, :], ident[:, :])
                    ins.then_inc(b0.full, 1)
                if live[2]:
                    for g in pair:
                        for kind, (b, use) in enumerate(((b6, "fa"), (b7, "fb"))):
                            bc[g][kind].wait_emptied(pe, i - 1, f"c{'ab'[kind]}{g}")
                            b.wait_free(pe, i, f"{use}{g}")
                            apart(pe, s_apart)
                            for h in range(H):
                                ins = per_tau(pe, b.t[:, h * D:(h + 1) * D], xexp[:, (g * 2 + kind) * H + h, :],
                                              rhs[par][g][:, kind * H + h, :])
                            ins.then_inc(b.full, 1)
                if live[2]:
                    for g in pair:
                        b6.wait_emptied(pe, i, f"fa{g}")
                        bz[g].wait_free(pe, i, f"z{g}")
                        apart(pe, s_apart)
                        for h in range(H):
                            ins = per_tau(pe, bz[g].t[:, h * D:(h + 1) * D], pexp[par][g][:, h, :], yf[g][:, h, :])
                        ins.then_inc(bz[g].full, 1)
                if live[1]:
                    for g in pair:
                        pe.wait_ge((s_xact, s_xpool)[g], i * 4 + 1)
                        for kind, (b, use) in enumerate(zip(by[g], ("ya", "yb"))):
                            b.wait_free(pe, i, f"{use}{g}")
                            apart(pe, s_apart)
                            for h in range(H):
                                ins = per_tau(pe, b.t[:, h * D:(h + 1) * D], xexp[:, (g * 2 + kind) * H + h, :],
                                              rhs[1 - par][g][:, kind * H + h, :])
                            ins.then_inc(b.full, 1)
                if live[0]:
                    for g in pair:
                        pe.wait_ge(s_yn, i * 2 + g + 1)
                        bn[g].wait_free(pe, i, f"pn{g}")
                        pe.transpose(bn[g].t[:, 0:128], yn[g][:, :], ident[:, :]).then_inc(bn[g].full, 1)
                    for g in pair:
                        bn[g].wait_emptied(pe, i, f"pn{g}")
                        b3.wait_free(pe, i, f"k{g}")
                        pe.matmul(b3.t[:, :], nT[g][:, :], wsT[:, HD:2 * HD], start=True, stop=True
                                  ).then_inc(b3.full, 1)
                        b1.wait_free(pe, i, f"be{g}")
                        pe.matmul(b1.t[:, 0:2 * H], nT[g][:, :], wsT[:, 5 * HD:], start=True, stop=True
                                  ).then_inc(b1.full, 1)
                        for b, use, k in ((b4, "r", 3), (b2, "q", 0), (b5, "v", 2), (b6, "w", 4)):
                            b.wait_free(pe, i, f"{use}{g}")
                            pe.matmul(b.t[:, :], nT[g][:, :], wsT[:, k * HD:(k + 1) * HD], start=True, stop=True
                                      ).then_inc(b.full, 1)
                if live[0]:
                    for g in pair:
                        for k, b, use in ((1, b3, "Tk"), (2, b4, "Tr"), (0, b2, "Tq")):
                            pe.wait_ge(s_kt, (i * 2 + g) * 3 + 3 + 1)
                            b.wait_free(pe, i, f"{use}{g}")
                            for hp in range(4):
                                ins = pe.transpose(b.t[:, hp * 128:(hp + 1) * 128],
                                                   kt[g][k][:, 2 * hp:2 * hp + 2, :].rearrange("p h d -> p (h d)"),
                                                   ident[:, :])
                            ins.then_inc(b.full, 1)
                        for b, use in ((b3, "Tk"), (b4, "Tr")):
                            b.wait_emptied(pe, i, f"{use}{g}")
                        for par_h, b in enumerate((b5, b6)):
                            b.wait_free(pe, i, f"A{g}")
                            apart(pe, s_apart)
                            rows = slice(D * par_h, D * par_h + D)
                            for kind in pair:
                                for hp in range(4):
                                    for a in pair:
                                        col = (kind * 4 + hp) * N
                                        own = kT[g][1 + kind][rows, hp, N * a:N * a + N]
                                        ins = pe.matmul(b.t[N * a:N * a + N, col:col + N], own, own,
                                                        start=True, stop=True)
                            ins.then_inc(b.full, 1)
                    b2.wait_emptied(pe, i, "Tq1")
                    for par_h, b in enumerate((b7, b1)):
                        b.wait_free(pe, i, "P")
                        apart(pe, s_apart)
                        rows = slice(D * par_h, D * par_h + D)
                        for g in pair:
                            for hp in range(4):
                                for a in pair:
                                    own = slice(N * a, N * a + N)
                                    col = (g * 4 + hp) * N
                                    ins = pe.matmul(b.t[own, col:col + N], kT[g][1][rows, hp, own],
                                                    kT[g][0][rows, hp, own], start=True, stop=True)
                        ins.then_inc(b.full, 1)
                if live[1]:
                    for g in pair:
                        for kind, (b, use) in enumerate(zip(bc[g], ("ca", "cb"))):
                            by[g][kind].wait_emptied(pe, i, f"y{'ab'[kind]}{g}")
                            b.wait_free(pe, i, f"{use}{g}")
                            apart(pe, s_apart)
                            for h in range(H):
                                ins = per_tau(pe, b.t[:, h * D:(h + 1) * D], cexp[1 - par][g][:, kind * H + h, :],
                                              yi[g][:, kind * H + h, :])
                            ins.then_inc(b.full, 1)
            pipeline(pe, step)

        def spread(eng, copy, i, solving, g, done):
            if solving:
                b7.wait_full(eng, i, "fb1")
            eng.wait_ge(s_xT, i + 1)
            apart(eng, s_apart)
            own = slice(g * 2 * H, (g + 1) * 2 * H)
            for blk in range(4):
                rows = slice(B * blk, B * blk + B)
                copy(xexp[rows, own, B * (blk % 2):B * (blk % 2) + B],
                     xT[rows, :, own].rearrange("p t u -> p u t")).then_inc(done, 1)

        @block.scalar
        def _(act):
            act.preload_act_table_set("natural_log_exp_and_others")
            act.wait_ge(s_zeroed, 7)
            PER = 6

            def step(i, par, live):
                chain = Tally(act, s_act, i * PER)
                if live[0]:
                    for g in pair:
                        ins = act.activation(hcol[g][:, :].rearrange("c (a n) -> c a n", a=2),
                                             hT[:, :, bass.ds(i * 4 + 2 * g, 2)].rearrange("c n a -> c a n"), ACT.Copy)
                    ins.then_inc(s_hcol, 1)
                if live[2]:
                    for g in pair:
                        for kind, (b, use) in enumerate(((b6, "fa"), (b7, "fb"))):
                            b.wait_full(act, i, f"{use}{g}")
                            if kind == 0:
                                act.wait_ge(y_stored[g], (i - 2) * 16 + 1)
                            act.activation(yf[g][:, kind * H:(kind + 1) * H, :].rearrange("p h d -> p (h d)"),
                                           b.t[:, :], ACT.Copy).then_inc(b.free, 1)
                if live[1]:
                    spread(act, lambda o, s: act.activation(o, s, ACT.Copy), i, live[2], 0, s_xact)

                def rsqrt(k, var, ready):
                    for g in pair:
                        act.wait_ge(var, i * 2 + g + 1)
                        chain.link(act.activation(rstd[g][:, 2 + k:3 + k], mv[g][:, 2 * k + 1:2 * k + 2],
                                                  ACT.Ln, bias=eps))
                        act.activation(rstd[g][:, k:k + 1], rstd[g][:, 2 + k:3 + k], ACT.Exp, scale=-0.5
                                       ).then_inc(ready, 1)

                def keep_y(g):
                    for kind, (b, use) in enumerate(zip(by[g], ("ya", "yb"))):
                        b.wait_full(act, i, f"{use}{g}")
                        act.activation(yi[g][:, kind * H:(kind + 1) * H, :].rearrange("p h d -> p (h d)"),
                                       b.t[:, :], ACT.Copy).then_inc(b.free, 1)
                if live[0]:
                    rsqrt(0, s_var1, s_rstd1)
                if live[2]:
                    for g in pair:
                        bz[g].wait_full(act, i, f"z{g}")
                        act.wait_ge(z_stored[g], (i - 2) * 16 + 1)
                        act.activation(zf[g][:, :, :].rearrange("p h d -> p (h d)"), bz[g].t[:, :], ACT.Copy
                                       ).then_inc(bz[g].free, 1)
                if live[0]:
                    rsqrt(1, s_var2, s_rstd2)
                if live[1]:
                    keep_y(0)
                if live[0]:
                    for g in pair:
                        bn[g].wait_full(act, i, f"pn{g}")
                        act.activation(nT[g][:, :], bn[g].t[:, 0:128], ACT.Identity, scale=gam[:, :], bias=bet[:, :]
                                       ).then_inc(bn[g].free, 1)
                if live[1]:
                    keep_y(1)
                if live[0]:
                    for g in pair:
                        b1.wait_emptied(act, i, f"be{g}")
                        chain.link(act.activation(sbeta[g][:, :], bcut[g][:, 0, :], ACT.Exp, scale=-1.0))
                        act.activation(sbeta[g][:, :], sbeta[g][:, :], ACT.Ln, bias=one).then_inc(s_blog, 1)
                        for k, b, use in ((1, b3, "k"), (2, b4, "r"), (0, b2, "q")):
                            b.wait_emptied(act, i, f"{use}{g}")
                            act.activation(ek[g][k][:, :, :], ek[g][k][:, :, :], ACT.Exp).then_inc(s_e, 1)
                            if k == 1:
                                act.wait_ge(s_bsum, i * 2 + g + 1)
                                act.activation(sbeta[g][:, :], sbeta[g][:, :], ACT.Exp, scale=-0.5
                                               ).then_inc(s_sbeta, 1)
                if live[0]:
                    for g in pair:
                        for k, b, use in ((1, b3, "Tk"), (2, b4, "Tr"), (0, b2, "Tq")):
                            b.wait_full(act, i, f"{use}{g}")
                            act.activation(kT[g][k][:, :, :].rearrange("p a b -> p (a b)"), b.t[:, :], ACT.Copy
                                           ).then_inc(b.free, 1)
                        for par_h, b in enumerate((b5, b6)):
                            b.wait_full(act, i, f"A{g}")
                            units = b.t[:, :].rearrange("p (u x) -> p u x", u=8)
                            linv = lin[:, :, :].rearrange("p x (g k v) -> p g v k x", g=2, v=2)
                            cv = cexp[par][g][:, :, :].rearrange("p (k v) x -> p v k x", v=2)
                            for blk in range(4):
                                rows = slice(B * blk, B * blk + B)
                                act.activation(linv[rows, g, par_h, :, :],
                                               units[rows, :, B * (blk % 2):B * (blk % 2) + B], ACT.Copy)
                            for a in pair:
                                rows = slice(N * a, N * a + B)
                                ins = act.activation(cv[rows, par_h, :, B:2 * B], units[rows, :, B:2 * B], ACT.Copy)
                            ins.then_inc(b.free, 1)
                    assert chain.n == PER
            pipeline(act, step)

        @block.vector
        def _(dve):
            MASK, SUBTRACT = (4, 5), (10, 15)
            dve.wait_ge(s_zeroed, 7)
            CB = B // 4
            PER = 2 * (3 + 2 * 4) + 2 * 6 + 1 + 2 * (B - 1) + 2 * (B - 1 - CB)

            def subtract(i, par, g):
                for kind, (b, use) in enumerate(zip(bc[g], ("ca", "cb"))):
                    b.wait_full(dve, i, f"{use}{g}")
                    right = rhs[1 - par][g][:, kind * H:(kind + 1) * H, :]
                    dve.tensor_tensor(right, right, b.t[:, :].rearrange("p (h d) -> p h d", h=H), ALU.subtract
                                      ).then_inc(b.free, 1)

            def step(i, par, live):
                chain = Tally(dve, s_dve, i * PER)
                if live[0]:
                    hrow = [b0.t[:, g * 128:g * 128 + C] for g in pair]
                    b0.wait_full(dve, i, "ph")
                    for g in pair:
                        chain.link(dve.bn_stats(stats[g][:, :], hrow[g]))
                        apart(dve, s_apart)
                        dve.bn_aggr(mv[g][:, 0:2], stats[g][:, :]).then_inc(s_var1, 1)
                    for g in pair:
                        dve.wait_ge(s_rstd1, i * 2 + g + 1)
                        newton(dve, chain, rstd[g][:, 0:1], mv[g][:, 1:2], stats[g])
                        chain.link(dve.tensor_scalar(yln[g][:, :], hrow[g], mv[g][:, 0:1], rstd[g][:, 0:1],
                                                     ALU.subtract, ALU.mult))
                        chain.link(dve.bn_stats(stats[g][:, :], yln[g][:, :]))
                        apart(dve, s_apart)
                        dve.bn_aggr(mv[g][:, 2:4], stats[g][:, :]).then_inc(s_var2, 1)
                    for g in pair:
                        dve.wait_ge(r_stored[g], i * 16 + 1)
                        ins = dve.tensor_tensor(res[g][:, :], hrow[g], yln[g][:, :], ALU.add)
                    ins.then_inc(b0.free, 1)
                    for g in pair:
                        dve.wait_ge(s_rstd2, i * 2 + g + 1)
                        newton(dve, chain, rstd[g][:, 1:2], mv[g][:, 3:4], stats[g])
                        dve.tensor_scalar(yn[g][:, :], yln[g][:, :], mv[g][:, 2:3], rstd[g][:, 1:2],
                                          ALU.subtract, ALU.mult).then_inc(s_yn, 1)
                    for g in pair:
                        b1.wait_full(dve, i, f"be{g}")
                        chain.link(dve.tensor_scalar(bcut[g][:, 0, :], b1.t[:, 0:2 * H], -CUT, None, ALU.max))
                        dve.tensor_tensor(bcut[g][:, 1, :], b1.t[:, 0:2 * H], bcut[g][:, 0, :], ALU.subtract
                                          ).then_inc(b1.free, 1)
                        softmaxes = ((1, b3, "k"), (2, b4, "r"), (0, b2, "q"))
                        for k, b, use in softmaxes:
                            b.wait_full(dve, i, f"{use}{g}")
                            chain(dve.tensor_reduce(nmax[:, k * H:(k + 1) * H],
                                                    b.t[:, :].rearrange("p (h d) -> p h d", h=H), AX.X, ALU.max,
                                                    negate=True))
                        chain.wait()
                        for k, b, use in softmaxes:
                            dve.tensor_tensor(ek[g][k][:, :, :], b.t[:, :].rearrange("p (h d) -> p h d", h=H),
                                              nmax[:, k * H:(k + 1) * H, None].broadcast_to([128, H, D]),
                                              ALU.add).then_inc(b.free, 1)
                        dve.wait_ge(s_sbeta, i * 2 + g + 1)
                        for kind, (b, use) in enumerate(((b5, "v"), (b6, "w"))):
                            b.wait_full(dve, i, f"{use}{g}")
                            dve.tensor_tensor(rhs[par][g][:, kind * H:(kind + 1) * H, :],
                                              b.t[:, :].rearrange("p (h d) -> p h d", h=H),
                                              sbeta[g][:, kind * H:(kind + 1) * H, None].broadcast_to([128, H, D]),
                                              ALU.mult).then_inc(b.free, 1)
                        for k in (1, 2, 0):
                            dve.wait_ge(s_e, (i * 2 + g) * 3 + (3, 1, 2)[k])
                            ins = dve.tensor_reduce(sums[g][:, k * H:(k + 1) * H], ek[g][k][:, :, :], AX.X, ALU.add)
                        chain.link(ins)
                        chain.link(dve.reciprocal(cc[g][:, :], sums[g][:, :]))
                        dve.tensor_tensor(cc[g][:, H:], cc[g][:, H:], sbeta[g][:, :], ALU.mult).then_inc(s_cc, 1)
                    b5.wait_emptied(dve, i, "A1")
                    b6.wait_emptied(dve, i, "A1")
                    chain.link(dve.transpose(lt[:, :, :], lin[:, :, :]))
                    dve.wait_ge(s_xi, i + 1)
                    done = [chain.n, chain.n]
                    for s in range(B - 1):
                        n = B - 1 - s
                        low = lt[:, s, s + 1:B]
                        cols = [slice(0, min(s + 1, CB))] + ([slice(CB, s + 1)] if s >= CB else [])
                        tmp = [prod[:, k, 0:n * (c.stop - c.start)].rearrange("p (r c) -> p r c", r=n)
                               for k, c in enumerate(cols)]
                        made = [0, 0]
                        for k, (c, to) in enumerate(zip(cols, tmp)):
                            chain.wait_for(done[k])
                            chain(dve.tensor_tensor(to, low[:, :, None].broadcast_to([128, n, c.stop - c.start]),
                                                    xi[:, s, c][:, None, :].broadcast_to([128, n, c.stop - c.start]),
                                                    ALU.mult))
                            made[k] = chain.n
                        if s in MASK:
                            par_h = MASK.index(s)
                            b = (b7, b1)[par_h]
                            b.wait_full(dve, i, "P")
                            for g in pair:
                                ins = dve.tensor_tensor(pexp[par][g][:, par_h::2, :],
                                                        b.t[:, g * 4 * N:(g + 1) * 4 * N].rearrange("p (h t) -> p h t", h=4),
                                                        mask[:, None, :].broadcast_to([128, 4, N]), ALU.mult)
                            ins.then_inc(b.free, 1)
                        if s in SUBTRACT and live[1]:
                            subtract(i, par, SUBTRACT.index(s))
                        for k, (c, to) in enumerate(zip(cols, tmp)):
                            chain.wait_for(made[k])
                            chain(dve.tensor_tensor(xi[:, s + 1:B, c], xi[:, s + 1:B, c], to, ALU.subtract))
                            done[k] = chain.n
                    chain.wait()
                    if live[1]:
                        dve.wait_ge(s_xact, i * 4 + 1)
                        dve.wait_ge(s_xpool, i * 4 + 1)
                    dve.transpose(xT[:, :, :], xi[:, :, :]).then_inc(s_xT, 1)
                    assert chain.n == PER
                elif live[1]:
                    for g in pair:
                        subtract(i, par, g)
            pipeline(dve, step)

        @block.gpsimd
        def _(pool):
            for r in pair:
                for g in pair:
                    pool.memset(cexp[r][g][:, :, :], 0.0).then_inc(s_zeroed, 1)
            pool.memset(xexp[:, :, :], 0.0).then_inc(s_zeroed, 1)
            pool.memset(xid[:, :, :], 0.0).then_inc(s_zeroed, 1)
            pool.wait_ge(s_zeroed, 6)
            pool.memset(xid[:, :, :].rearrange("p a b -> p (a b)")[:, 0::B + 1], 1.0).then_inc(s_zeroed, 1)
            pool.wait_ge(s_zeroed, 7)

            def step(i, par, live):
                if live[1]:
                    spread(pool, pool.tensor_copy, i, live[2], 1, s_xpool)
                    pool.wait_ge(s_xpool, i * 4 + 1)
                if live[0]:
                    for g in pair:
                        pool.wait_ge(s_blog, i * 2 + g + 1)
                        pool.tensor_tensor(sbeta[g][:, :], sbeta[g][:, :], bcut[g][:, 1, :], ALU.subtract
                                           ).then_inc(s_bsum, 1)
                        pool.wait_ge(s_cc, i * 2 + g + 1)
                        pool.wait_ge(k_stored[g], i * 16 + 1)
                        for k in (1, 2, 0):
                            pool.tensor_tensor(kt[g][k][:, :, :], ek[g][k][:, :, :],
                                               cc[g][:, k * H:(k + 1) * H, None].broadcast_to([128, H, D]), ALU.mult
                                               ).then_inc(s_kt, 1)
                    pool.wait_ge(s_xT, i + 1)
                    apart(pool, s_apart)
                    pool.tensor_copy(xi[:, :, :], xid[:, :, :]).then_inc(s_xi, 1)
            pipeline(pool, step)


def recurrence(nc, k_scr, y_scr, z_scr, ident):
    RING = 2
    ROWS = 16

    def shared_products(n):
        return n // 3 if n >= 8 else 0

    def shared_scalings(n):
        return n * 3 // 10 if n >= 4 else 0

    with ExitStack() as c:
        def sb(name, shape, dt=F32):
            return c.enter_context(nc.sbuf_tensor(name, shape, dt))

        def sem(name):
            return c.enter_context(nc.semaphore(name))
        heads = range(HP)
        ring = range(RING)
        ks = sb("ks", [TT, N, HP, D])
        ys = sb("ys", [TT, N, HP, D])
        zr = [sb(f"zring{r}", [TT, HP, 2, D]) for r in ring]
        hr = [sb(f"hring{r}", [TT, HP, D]) for r in ring]
        prod = [sb(f"rprod{h}", [TT, N, D]) for h in heads]
        nm = [sb(f"nm{h}", [TT, 1]) for h in heads]
        den = [sb(f"den{h}", [TT, 2]) for h in heads]
        coef = [sb(f"coef{h}", [TT, N]) for h in heads]
        h0 = sb("h0", [TT, D])
        dots = [c.enter_context(nc.psum_tensor(f"dots{h}", [128, 512], F32)) for h in heads]
        expo = [sb(f"expo{h}", [TT, D]) for h in heads]
        ph = [c.enter_context(nc.psum_tensor(f"hsum{h}", [128, 512], F32)) for h in heads]
        s_h0, s_end, s_apart = sem("h0_set"), sem("pass_ended"), sem("waited")
        s_k = [sem(f"k_loaded{r}") for r in range(N // ROWS)]
        s_y = [sem(f"y_loaded{r}") for r in range(N // ROWS)]
        s_z = [sem(f"z_loaded{r}") for r in ring]
        s_st = [sem(f"h_stored{r}") for r in ring]
        s_max, s_exp, s_fold, s_dve, s_part, s_dots, s_coef, s_mix, s_amix, s_h = (
            [sem(f"{n}{h}") for h in heads] for n in
            "max_ready exp_ready h_folded rec_dve products_shared dots_ready coef_ready mix_ready act_mix_ready "
            "h_ready".split())

        def parts(t):
            return sum(shared_products(u + 1) > 0 for u in range(t + 1))

        def mixes(t):
            return sum(shared_scalings(u + 1) > 0 for u in range(t + 1))
        PARTS, MIXES = parts(N - 1), mixes(N - 1)
        NPASS = H // HP
        LR = N // RING
        block = c.enter_context(nc.Block())

        @block.sync
        def _(sp):
            for r in ring:
                sp.sem_inc(s_st[r], 1)
            sp.sem_inc(s_end, 1)
            with sp.Fori(0, NPASS) as p:
                cols = bass.ds(p * (HP * D), HP * D)
                sp.wait_ge(s_end, p + 1)
                apart(sp, s_apart)

                def load_z(t):
                    sp.dma_start(zr[t % RING][:, :, 0, :], z_scr[0:TT, t, cols].rearrange("p (h d) -> p h d", h=HP)
                                 ).then_inc(s_z[t % RING], 16)
                for t in range(RING):
                    load_z(t)
                for r in range(N // ROWS):
                    part = slice(r * ROWS, (r + 1) * ROWS)
                    for dst, src, done in ((ks, k_scr, s_k), (ys, y_scr, s_y)):
                        sp.dma_start(dst[:, part, :, :].rearrange("p n h d -> p n (h d)"), src[0:TT, part, cols]
                                     ).then_inc(done[r], 16)
                for t in range(N):
                    for h in heads:
                        sp.wait_ge(s_fold[h], p * N + t + 1)
                    apart(sp, s_apart)
                    sp.dma_start(z_scr[0:TT, t, cols], hr[t % RING][:, :, :].rearrange("p h d -> p (h d)")
                                 ).then_inc(s_st[t % RING], 16)
                    if t + RING < N:
                        load_z(t + RING)
            for r in ring:
                sp.wait_ge(s_st[r], 16 * LR * NPASS + 1)

        @block.scalar
        def _(act):
            act.preload_act_table_set("natural_log_exp_and_others")
            act.wait_ge(s_h0, 1 + RING)
            slots = [(t, h) for t in range(N) for h in heads]
            with act.Fori(0, NPASS) as p:
                def exponentials(t, h):
                    act.wait_ge(s_max[h], p * N + t + 1)
                    src = hr[(t - 1) % RING][:, h, :] if t else h0[:, :]
                    act.activation(expo[h][:, :], src, ACT.Exp, bias=nm[h][:, :],
                                   accum_out=den[h][:, 0:1]).then_inc(s_exp[h], 1)
                exponentials(*slots[0])
                for k, (t, h) in enumerate(slots):
                    n = t + 1
                    if k + 1 < len(slots):
                        exponentials(*slots[k + 1])
                    if t % ROWS == 0 and h == 0:
                        act.wait_ge(s_y[t // ROWS], p * 16 + 16)
                    act.wait_ge(s_dots[h], p * N + n)
                    act.activation(coef[h][:, 0:n], dots[h][0:TT, 0:n], ACT.Identity, scale=den[h][:, 1:2],
                                   bias=h0[:, 0:1]).then_inc(s_coef[h], 1)
                    act.wait_ge(s_coef[h], p * N + n)
                    for s in range(n - shared_scalings(n), n):
                        ins = act.activation(prod[h][:, s, :], ys[:, s, h, :], ACT.Identity,
                                             scale=coef[h][:, s:s + 1], bias=h0[:, 0:1])
                    if shared_scalings(n):
                        ins.then_inc(s_amix[h], 1)

        @block.vector
        def _(dve):
            dve.memset(h0[:, :], 0.0).then_inc(s_h0, 1)
            for r in ring:
                dve.memset(zr[r][:, :, 1, :], 0.0).then_inc(s_h0, 1)
            dve.wait_ge(s_h0, 1 + RING)
            with dve.Fori(0, NPASS) as p:
                steps = [Tally(dve, s_dve[h], p * (2 * N)) for h in heads]
                slots = [(t, h) for t in range(N) for h in heads]

                def fold(t, h):
                    dve.wait_ge(s_h[h], p * N + t + 1)
                    if h == 0:
                        dve.wait_ge(s_st[t % RING], p * (16 * LR) + 16 * (t // RING) + 1)
                    dve.tensor_reduce(hr[t % RING][:, h, :],
                                      ph[h][0:TT, 0:2 * D].rearrange("p (a d) -> p d a", a=2) if t else
                                      ph[h][0:TT, 0:D].rearrange("p (a d) -> p d a", a=1), AX.X, ALU.add
                                      ).then_inc(s_fold[h], 1)

                def find_max(t, h):
                    src = h0[:, :]
                    if t:
                        fold(t - 1, h)
                        dve.wait_ge(s_fold[h], p * N + t)
                        src = hr[(t - 1) % RING][:, h, :]
                    dve.tensor_reduce(nm[h][:, :], src, AX.X, ALU.max, negate=True).then_inc(s_max[h], 1)

                find_max(*slots[0])
                for k, (t, h) in enumerate(slots):
                    n = t + 1
                    step = steps[h]
                    if k + 1 < len(slots):
                        find_max(*slots[k + 1])
                    if t % ROWS == 0 and h == 0:
                        dve.wait_ge(s_k[t // ROWS], p * 16 + 16)
                    dve.wait_ge(s_exp[h], p * N + n)
                    step(dve.reciprocal(den[h][:, 1:2], den[h][:, 0:1]))
                    own = n - shared_products(n)
                    step.link(dve.tensor_tensor(prod[h][:, 0:own, :], ks[:, 0:own, h, :],
                                                expo[h][:, None, :].broadcast_to([TT, own, D]), ALU.mult))
                    if own < n:
                        dve.wait_ge(s_part[h], p * PARTS + parts(t))
                    dve.tensor_reduce(dots[h][0:TT, 0:n], prod[h][:, 0:n, :], AX.X, ALU.add).then_inc(s_dots[h], 1)
                for h in heads:
                    fold(N - 1, h)
                assert all(s.n == 2 * N for s in steps)

        @block.gpsimd
        def _(pool):
            with pool.Fori(0, NPASS) as p:
                slots = [(t, h) for t in range(N) for h in heads]

                def products(t, h):
                    n = t + 1
                    own = n - shared_products(n)
                    if own < n:
                        if t % ROWS == 0 and h == 0:
                            pool.wait_ge(s_k[t // ROWS], p * 16 + 16)
                        pool.wait_ge(s_exp[h], p * N + n)
                        pool.tensor_tensor(prod[h][:, own:n, :], ks[:, own:n, h, :],
                                           expo[h][:, None, :].broadcast_to([TT, n - own, D]), ALU.mult
                                           ).then_inc(s_part[h], 1)
                for k, (t, h) in enumerate(slots):
                    n = t + 1
                    if k + 1 < len(slots):
                        products(*slots[k + 1])
                    if t % ROWS == 0 and h == 0:
                        pool.wait_ge(s_y[t // ROWS], p * 16 + 16)
                    pool.wait_ge(s_coef[h], p * N + n)
                    own = n - shared_scalings(n)
                    pool.tensor_tensor(prod[h][:, 0:own, :], ys[:, 0:own, h, :],
                                       coef[h][:, 0:own, None].broadcast_to([TT, own, D]), ALU.mult
                                       ).then_inc(s_mix[h], 1)

        @block.tensor
        def _(pe):
            pe.wait_ge(s_h0, 1 + RING)
            with pe.Fori(0, NPASS) as p:
                for t in range(N):
                    for h in heads:
                        pe.wait_ge(s_z[t % RING], p * (16 * LR) + 16 * (t // RING) + 16)
                        if t:
                            pe.wait_ge(s_fold[h], p * N + t)
                        pe.matmul(ph[h][0:TT, 0:2 * D], ident[0:TT, 0:TT],
                                  zr[t % RING][:, h, :, :].rearrange("p a d -> p (a d)"), start=True, stop=False)
                        pe.wait_ge(s_mix[h], p * N + t + 1)
                        if shared_scalings(t + 1):
                            pe.wait_ge(s_amix[h], p * MIXES + mixes(t))
                        for s in range(0, t + 1, 2):
                            m = min(2, t + 1 - s)
                            ins = pe.matmul(ph[h][0:TT, 0:m * D], ident[0:TT, 0:TT],
                                            prod[h][:, s:s + m, :].rearrange("p s d -> p (s d)"),
                                            start=False, stop=(s + m == t + 1))
                        ins.then_inc(s_h[h], 1)
                for h in heads:
                    pe.wait_ge(s_fold[h], p * N + N)
                pe.sem_inc(s_end, 1)


def finish(nc, v):
    ident, identb, ones, woT, wq, wmax, eps = (v[k] for k in "ident identb ones woT wq wmax eps".split())
    z_scr, out = v["z_scr"], v["out"]
    NTT = TT // 2
    with ExitStack() as c:
        def sb(name, shape, dt=F32):
            return c.enter_context(nc.sbuf_tensor(name, shape, dt))

        def sem(name):
            return c.enter_context(nc.semaphore(name))
        LB = 3
        assert NTT % LB == 0
        trio = range(LB)
        rows = [sb(f"hrows{b}", [128, HD]) for b in trio]
        hT = [sb(f"hsT{b}", [128, 4, 128]) for b in trio]
        stats = [sb(f"fstats{b}", [128, 6]) for b in trio]
        mv = sb("fmv", [128, LB, 2])
        rstd, lnv, tmp = (sb(name, [128, LB]) for name in ("frstd", "flnv", "fnewton"))
        big = sb("big", [128, NTT])
        ln = sb("ln", [128, NTT, C])
        res = sb("res", [128, NTT, C])
        s_res = sem("res_in")
        amax = sb("amax", [128, 8])
        q = sb("q", [128, 3, LB * C])
        qb = sb("qb", [128, LB, C], BF16)
        qT = [sb(f"qT{b}", [C, 128], BF16) for b in trio]
        fin = [sb(f"fin{b}", [128, C]) for b in trio]
        pt = [c.enter_context(nc.psum_tensor(f"pt{b}", [128, 512], F32)) for b in trio]
        po = [c.enter_context(nc.psum_tensor(f"po{b}", [128, 512], F32)) for b in trio]
        pg = c.enter_context(nc.psum_tensor("pg", [128, 512], F32))
        s_in = [sem(f"rows_in{b}") for b in trio]
        s_out = [sem(f"stored{b}") for b in trio]
        s_apart, s_t, s_hT, s_o, s_h2, s_var, s_rstd, s_act, s_dve, s_ln, s_a, s_b = (sem(s) for s in (
            "waited rows_turned hsT_ready product_ready h2_ready fvar_ready frstd_ready fact_step fdve_step ln_ready "
            "amax_turned amax_spread").split())
        with nc.Block() as block:
            @block.sync
            def _(sp):
                sp.dma_start(res[:, :, :], v["res_scr"][0:TT, :, :].rearrange("(j a) n c -> (a n) j c", a=2)
                             ).then_inc(s_res, 16)
                with sp.Fori(0, NTT // LB) as i:
                    for b in trio:
                        sp.wait_ge(s_t, i * LB + 1)
                        apart(sp, s_apart)
                        sp.dma_start(rows[b][:, :], z_scr[bass.ds(i * (2 * LB) + 2 * b, 2), :, :]
                                     .rearrange("a n c -> (a n) c")).then_inc(s_in[b], 16)

            @block.tensor
            def _(pe):
                for s in (s_t, s_hT, s_h2, s_o):
                    pe.sem_inc(s, 1)
                with pe.Fori(0, NTT // LB) as i:
                    for b in trio:
                        pe.wait_ge(s_in[b], i * 16 + 16)
                        pe.wait_ge(s_hT, i * LB + 1)
                        for k in range(4):
                            ins = pe.transpose(pt[b][:, k * 128:(k + 1) * 128], rows[b][:, k * 128:(k + 1) * 128],
                                               ident[:, :])
                        ins.then_inc(s_t, 1)
                    for b in trio:
                        pe.wait_ge(s_hT, i * LB + b + 1 + 1)
                        pe.wait_ge(s_h2, i * LB + 1)
                        for k in range(4):
                            ins = pe.matmul(po[b][:, 0:C], hT[b][:, k, :], woT[:, k, :], start=(k == 0), stop=(k == 3))
                        ins.then_inc(s_o, 1)

            @block.scalar
            def _(act):
                act.preload_act_table_set("natural_log_exp_and_others")
                with act.Fori(0, NTT // LB) as i:
                    for b in trio:
                        act.wait_ge(s_t, i * LB + b + 1 + 1)
                        act.wait_ge(s_o, i * LB + 1)
                        act.activation(hT[b][:, :, :].rearrange("p a b -> p (a b)"), pt[b][:, :], ACT.Copy
                                       ).then_inc(s_hT, 1)
                    act.wait_ge(s_var, i * LB + LB)
                    act.activation(lnv[:, :], mv[:, :, 1], ACT.Ln, bias=eps).then_inc(s_act, 1)
                    act.wait_ge(s_act, i + 1)
                    act.activation(rstd[:, :], lnv[:, :], ACT.Exp, scale=-0.5).then_inc(s_rstd, 1)

            @block.vector
            def _(dve):
                dve.wait_ge(s_res, 16)
                with dve.Fori(0, NTT // LB) as i:
                    step = Tally(dve, s_dve, i * (LB + 5))
                    for b in trio:
                        h2 = res[:, bass.ds(i * LB + b, 1), :].rearrange("p a c -> p (a c)")
                        dve.wait_ge(s_o, i * LB + b + 1 + 1)
                        dve.tensor_tensor(h2, po[b][:, 0:C], h2, ALU.add).then_inc(s_h2, 1)
                        dve.wait_ge(s_h2, i * LB + b + 1 + 1)
                        apart(dve, s_apart)
                        step.link(dve.bn_stats(stats[b][:, :], h2))
                        apart(dve, s_apart)
                        dve.bn_aggr(mv[:, b, :], stats[b][:, :]).then_inc(s_var, 1)
                    dve.wait_ge(s_rstd, i + 1)
                    step(dve.tensor_scalar(lnv[:, :], mv[:, :, 1], EPS, -0.5, ALU.add, ALU.mult))
                    step.link(dve.tensor_tensor(tmp[:, :], rstd[:, :], rstd[:, :], ALU.mult))
                    step.link(dve.tensor_tensor(tmp[:, :], tmp[:, :], lnv[:, :], ALU.mult))
                    step.link(dve.tensor_scalar(tmp[:, :], tmp[:, :], 1.5, None, ALU.add))
                    step.link(dve.tensor_tensor(rstd[:, :], rstd[:, :], tmp[:, :], ALU.mult))
                    for b in trio:
                        h2 = res[:, bass.ds(i * LB + b, 1), :].rearrange("p a c -> p (a c)")
                        y = ln[:, bass.ds(i * LB + b, 1), :].rearrange("p a c -> p (a c)")
                        dve.tensor_scalar(y, h2, mv[:, b, 0:1], rstd[:, b:b + 1], ALU.subtract, ALU.mult
                                          ).then_inc(s_ln, 1)
                    dve.wait_ge(s_ln, i * LB + LB)
                    dve.tensor_reduce(big[:, bass.ds(i * LB, LB)], ln[:, bass.ds(i * LB, LB), :], AX.X, ALU.max,
                                      apply_absolute_value=True)
                    assert step.n == LB + 5

        s_qt, s_qT, s_p, s_f, s_e, s_c = (sem(s) for s in (
            "q_turned qT_ready linear_ready fin_ready e_step chain_step").split())
        with nc.Block() as block:
            @block.tensor
            def _(pe):
                for s in (s_qT, s_f, s_p, *s_out):
                    pe.sem_inc(s, 1)
                pe.wait_ge(s_c, 1)
                pe.transpose(pg[0:1, 0:128], amax[:, 0:1], ident[:, :]).then_inc(s_a, 1)
                pe.wait_ge(s_c, 2)
                pe.matmul(pg[:, 128:129], ones[0:1, :], amax[0:1, 1:2], start=True, stop=True).then_inc(s_b, 1)
                with pe.Fori(0, NTT // LB) as i:
                    for b in trio:
                        pe.wait_ge(s_e, i * 6 + 6)
                        pe.wait_ge(s_qT, i * LB + 1)
                        pe.transpose(pt[b][:, 0:64].bitcast(BF16), qb[:, b, :], identb[:, :]).then_inc(s_qt, 1)
                    for b in trio:
                        pe.wait_ge(s_qT, i * LB + b + 1 + 1)
                        pe.wait_ge(s_f, i * LB + 1)
                        pe.matmul(po[b][:, 0:C], qT[b][:, :], wq[:, :], start=True, stop=True).then_inc(s_p, 1)

            @block.scalar
            def _(act):
                act.preload_act_table_set("natural_log_exp_and_others")
                with act.Fori(0, NTT // LB) as i:
                    for b in trio:
                        act.wait_ge(s_qt, i * LB + b + 1)
                        act.wait_ge(s_p, i * LB + 1)
                        act.activation(qT[b][:, :], pt[b][:, 0:64].bitcast(BF16), ACT.Copy).then_inc(s_qT, 1)

            @block.vector
            def _(dve):
                step = Tally(dve, s_c)
                step(dve.tensor_reduce(amax[:, 0:1], big[:, :], AX.X, ALU.max))
                dve.wait_ge(s_a, 1)
                step(dve.tensor_reduce(amax[0:1, 1:2], pg[0:1, 0:128], AX.X, ALU.max))
                dve.wait_ge(s_b, 1)
                step.link(dve.tensor_scalar(amax[:, 2:3], pg[:, 128:129], 1e-12, None, ALU.max))
                step.link(dve.reciprocal(amax[:, 3:4], amax[:, 2:3]))
                step.link(dve.tensor_scalar(amax[:, 3:4], amax[:, 3:4], FP8_MAX, None, ALU.mult))
                step.link(dve.tensor_scalar(amax[:, 4:5], amax[:, 2:3], 1.0 / FP8_MAX, None, ALU.mult))
                step.link(dve.tensor_scalar(amax[:, 5:6], wmax[:, :], 1.0 / FP8_MAX, None, ALU.mult))
                step.link(dve.tensor_tensor(amax[:, 6:7], amax[:, 4:5], amax[:, 5:6], ALU.mult))
                with dve.Fori(0, NTT // LB) as i:
                    step = Tally(dve, s_e, i * 6)
                    quantise(dve, step, qb[:, :, :].rearrange("p a c -> p (a c)"),
                             ln[:, bass.ds(i * LB, LB), :].rearrange("p a c -> p (a c)"), amax[:, 3:4], q)
                    for b in trio:
                        h2 = res[:, bass.ds(i * LB + b, 1), :].rearrange("p a c -> p (a c)")
                        dve.wait_ge(s_p, i * LB + b + 1 + 1)
                        dve.wait_ge(s_out[b], i * 32 + 1)
                        dve.scalar_tensor_tensor(out=fin[b][:, :], in0=po[b][:, 0:C], scalar=amax[:, 6:7], in1=h2,
                                                 op0=ALU.mult, op1=ALU.add).then_inc(s_f, 1)
                    assert step.n == 6

            @block.sync
            def _(sp):
                with sp.Fori(0, NTT // LB) as i:
                    for b in trio:
                        sp.wait_ge(s_f, i * LB + b + 1 + 1)
                        apart(sp, s_apart)
                        for a in range(2):
                            sp.dma_start(out[:, bass.ds(i * (2 * LB) + 2 * b + a, 1), :].rearrange("n a c -> (a n) c"),
                                         fin[b][N * a:N * a + N, :]).then_inc(s_out[b], 16)
                for b in trio:
                    sp.wait_ge(s_out[b], 32 * (NTT // LB) + 1)


_INS = ["x", "L0_tok_Wf", "L0_tok_bf", "L0_tok_Wi", "L0_tok_bi", "L0_tok_Wh", "L0_tok_bh", "L0_attn_W_slow",
        "L0_attn_W_out", "L0_attn_ln_gamma", "L0_attn_ln_beta", "L0_ffn_weight"]


def kernel(**inputs):
    import numpy as np
    import concourse.bacc as bacc
    from concourse.bass_utils import run_bass_kernel_spmd

    nc = bacc.Bacc("TRN2", target_bir_lowering=False, num_devices=1)
    arrays, args = {}, []
    for name in _INS:
        a = np.ascontiguousarray(inputs[name])
        arrays[f"in_{name}"] = a
        args.append(nc.dram_tensor(f"in_{name}", a.shape, mybir.dt.from_np(a.dtype), kind="ExternalInput").ap())
    out = nc.dram_tensor("out", (N, TT, C), F32, kind="ExternalOutput").ap()
    audio_layer(nc, *args, out)
    return run_bass_kernel_spmd(nc, [arrays], core_ids=[0]).results[0]["out"]
```
